# Optimizing a Trainium2 kernel written in Bass

```python
import numpy as np
import jax
import jax.numpy as jnp

def _softmax(x, axis=-1):
    return jax.nn.softmax(x, axis=axis)

def _gelu(x):
    return jax.nn.gelu(x, approximate=True)

def _silu(x):
    return jax.nn.silu(x)

def _sigmoid(x):
    return jax.nn.sigmoid(x)

def _layernorm(x, axis=-1, eps=1e-05):
    m = jnp.mean(x, axis=axis, keepdims=True)
    v = jnp.var(x, axis=axis, keepdims=True)
    return (x - m) / jnp.sqrt(v + eps)

def _scatter_add(tgt, idx, src, axis=0):
    return tgt.at[idx].add(src)

def _segment_sum(src, seg, n):
    return jax.ops.segment_sum(src, seg, n)
kernel_name = 'mk_gnn_resnorm_d2_gnn_r64_ab9b79'

def setup_inputs(seed: int=0):
    np.random.seed(seed)
    _w = jnp.asarray

    def _rec_inputs():
        import jax
        import jax.numpy as jnp
        _gk = jax.random.key(seed)
        x = -0.0005121 + 1.001 * jax.random.normal(jax.random.fold_in(_gk, 1), (100000, 64), jnp.float32)
        src = jax.random.randint(jax.random.fold_in(_gk, 2), (50000,), 0, 100000, jnp.int32)
        dst = jax.random.randint(jax.random.fold_in(_gk, 3), (50000,), 0, 100000, jnp.int32)
        _o = jnp.argsort(dst, stable=True)
        src = src[_o]
        dst = dst[_o]
        edge_attr_64 = -9.77346e-05 + 0.999888 * jax.random.normal(jax.random.fold_in(_gk, 12), (50000, 64), jnp.float32)
        edge_weight = jax.random.uniform(jax.random.fold_in(_gk, 14), (50000,), jnp.float32, 0.0, 1)
        edge_weight_n2 = jax.random.uniform(jax.random.fold_in(_gk, 15), (50000,), jnp.float32, 0.0, 1)
        return (x, src, dst, edge_attr_64, edge_weight, edge_weight_n2)
    x, src, dst, edge_attr_64, edge_weight, edge_weight_n2 = _rec_inputs()

    def _L0_gnn_setup():
        import jax, jax.numpy as jnp
        import numpy as np
        N_NODES = 50000
        N_EDGES = 12500
        D_NODE = 64
        D_EDGE = 64
        HIDDEN = 128
        key = jax.random.key(seed)
        k1, k2, k3, k4, k5 = jax.random.split(key, 5)
        x_node = jax.random.normal(k1, (N_NODES, D_NODE), dtype=jnp.float32)
        x_edge = jax.random.normal(k2, (N_EDGES, D_EDGE), dtype=jnp.float32)
        edge_index = jax.random.randint(k3, (2, N_EDGES), 0, N_NODES, dtype=jnp.int64)
        d_in = D_NODE + D_EDGE
        W1 = jax.random.normal(k4, (d_in, HIDDEN), dtype=jnp.float32) / np.sqrt(d_in)
        b1 = jnp.zeros((HIDDEN,), dtype=jnp.float32)
        W2 = jax.random.normal(k5, (HIDDEN, D_NODE), dtype=jnp.float32) / np.sqrt(HIDDEN)
        b2 = jnp.zeros((D_NODE,), dtype=jnp.float32)
        return {'x_node': x_node, 'x_edge': x_edge, 'edge_index': edge_index, 'W1': W1, 'b1': b1, 'W2': W2, 'b2': b2}
    _L0_gnn_all = _L0_gnn_setup()
    _L0_gnn_in = {k: v for k, v in _L0_gnn_all.items() if k in ('W1', 'b1', 'W2', 'b2')}
    del _L0_gnn_all

    def _L1_gnn_setup():
        import jax, jax.numpy as jnp
        import numpy as np
        from jax.ops import segment_sum
        N = 100000
        P = 25000
        F = 64
        H = 4
        FH = F // H
        key = jax.random.key(seed)
        ks = jax.random.split(key, 8)
        x = jax.random.normal(ks[0], (N, F), dtype=jnp.float32)
        phi_r_cut = jax.random.uniform(ks[1], (P,), dtype=jnp.float32)
        idx_i = jnp.sort(jax.random.randint(ks[2], (P,), 0, N))
        idx_j = jax.random.randint(ks[3], (P,), 0, N)
        pair_mask = jnp.ones((P,), dtype=jnp.float32)
        s = 1.0 / np.sqrt(FH)
        Wq = jax.random.uniform(ks[4], (H, FH, FH), jnp.float32, -s, s)
        Wk = jax.random.uniform(ks[5], (H, FH, FH), jnp.float32, -s, s)
        Wv = jax.random.uniform(ks[6], (H, FH, FH), jnp.float32, -s, s)
        return {'x': x, 'phi_r_cut': phi_r_cut, 'idx_i': idx_i, 'idx_j': idx_j, 'pair_mask': pair_mask, 'Wq': Wq, 'Wk': Wk, 'Wv': Wv}
    _L1_gnn_all = _L1_gnn_setup()
    _L1_gnn_in = {k: v for k, v in _L1_gnn_all.items() if k in ('Wq', 'Wk', 'Wv')}
    del _L1_gnn_all
    return {'x': x, 'src': src, 'dst': dst, 'edge_attr_64': edge_attr_64, 'edge_weight': edge_weight, 'edge_weight_n2': edge_weight_n2, 'L0_gnn_W1': _L0_gnn_in['W1'], 'L0_gnn_b1': _L0_gnn_in['b1'], 'L0_gnn_W2': _L0_gnn_in['W2'], 'L0_gnn_b2': _L0_gnn_in['b2'], 'L1_gnn_Wq': _L1_gnn_in['Wq'], 'L1_gnn_Wk': _L1_gnn_in['Wk'], 'L1_gnn_Wv': _L1_gnn_in['Wv']}

def reference(x, src, dst, edge_attr_64, edge_weight, edge_weight_n2, L0_gnn_W1, L0_gnn_b1, L0_gnn_W2, L0_gnn_b2, L1_gnn_Wq, L1_gnn_Wk, L1_gnn_Wv):
    import jax
    import jax.numpy as jnp

    def _L0_gnn_ref(x_node, x_edge, edge_index, W1, b1, W2, b2):
        import jax, jax.numpy as jnp
        import numpy as np
        N_NODES = 50000
        N_EDGES = 12500
        D_NODE = 64
        D_EDGE = 64
        HIDDEN = 128
        agg = jnp.zeros((x_node.shape[0], x_edge.shape[1]), dtype=x_edge.dtype)
        agg = agg.at[edge_index[0]].add(x_edge)
        agg = agg.at[edge_index[1]].add(x_edge)
        h = jnp.concatenate([x_node, agg], axis=1)
        h = jax.nn.relu(h @ W1 + b1)
        x_node_ = h @ W2 + b2
        return x_node_

    def _L1_gnn_ref(x, phi_r_cut, idx_i, idx_j, pair_mask, Wq, Wk, Wv):
        import jax, jax.numpy as jnp
        import numpy as np
        from jax.ops import segment_sum
        N = 100000
        P = 25000
        F = 64
        H = 4
        FH = F // H
        n, f = x.shape
        x_heads = x.reshape(n, H, FH)
        q = jnp.einsum('nhf,hfg->nhg', x_heads, Wq)
        k = jnp.einsum('nhf,hfg->nhg', x_heads, Wk)
        v = jnp.einsum('nhf,hfg->nhg', x_heads, Wv)
        alpha = (q[idx_j] * k[idx_j]).sum(axis=-1) / jnp.sqrt(jnp.asarray(FH, x.dtype))
        alpha = alpha * (pair_mask * phi_r_cut)[:, None]
        msg = alpha[:, :, None] * v[idx_j]
        out = segment_sum(msg, segment_ids=idx_i, num_segments=n)
        return out.reshape(n, f)
    edge_index = jnp.stack([src, dst])
    x = _layernorm(x + _L0_gnn_ref(x, edge_attr_64, edge_index, L0_gnn_W1, L0_gnn_b1, L0_gnn_W2, L0_gnn_b2), axis=-1)
    x = _layernorm(x + _L1_gnn_ref(x, edge_weight, src, dst, edge_weight_n2, L1_gnn_Wq, L1_gnn_Wk, L1_gnn_Wv), axis=-1)
    return x

_drawn_inputs = setup_inputs


def setup_inputs(seed=0):
    import zlib

    import numpy as np

    out = dict(_drawn_inputs(seed))
    spreads = {'L0_gnn_b1': (0.0, 0.1), 'L0_gnn_b2': (0.0, 0.1)}
    factors = {}
    for name, (base, spread) in spreads.items():
        noise = np.random.default_rng([zlib.crc32(name.encode()), seed]).standard_normal(out[name].shape)
        drawn = base * np.exp(spread * noise) if base else spread * noise
        out[name] = jnp.asarray(drawn.astype(out[name].dtype))
    for name, factor in factors.items():
        out[name] = (out[name] * factor).astype(out[name].dtype)
    return out
```

```python
from contextlib import ExitStack

import concourse.bass as bass
from concourse import mybir

F32 = mybir.dt.float32
I32 = mybir.dt.int32
ALU = mybir.AluOpType
ACT = mybir.ActivationFunctionType
AX_X = mybir.AxisListType.X

P = 128
G = 3
C = 10
GROUPS = [(0, 4), (4, 4), (8, 2)]
EPS = 1e-5


def build(nc, x, src, dst, edge_attr, edge_w, edge_w2, W1, b1, W2, b2, Wq, Wk, Wv, out):
    N, F = x.shape
    E = edge_attr.shape[0]
    HID = W1.shape[1]
    HEADS, FH, _ = Wq.shape

    T = E // P // (2 * G) * (2 * G)
    TAIL = E - P * T
    SB = T // G
    assert SB % 2 == 0 and 0 < TAIL <= P and T % G == 0
    CHUNKS = N // P // (2 * C) * 2
    COLS = CHUNKS * C
    REST = (N - P * COLS) // C
    assert REST * C == N - P * COLS and 0 < REST <= 32
    SPARE = G * P
    CF = C * F

    agg_src = nc.dram_tensor("agg_src", (N + SPARE, F), F32).ap()
    agg_dst = nc.dram_tensor("agg_dst", (N + SPARE, F), F32).ap()
    agg = [agg_src, agg_dst]
    x1 = nc.dram_tensor("x1", (N, F), F32).ap()
    acc = nc.dram_tensor("acc", (N + SPARE, F), F32).ap()

    def main_nodes(a):
        return a[0:P * COLS, :].rearrange("(p j) f -> p (j f)", p=P)

    def rest_nodes(a):
        return a[P * COLS:N, :].rearrange("(p j) f -> p (j f)", p=REST)

    def is_rest(q):
        return isinstance(q, int) and q == CHUNKS

    def rows(q):
        return REST if is_rest(q) else P

    def chunk_of(a, q):
        return rest_nodes(a) if is_rest(q) else main_nodes(a)[:, bass.ds(q * CF, CF)]

    def is_tail(k):
        return isinstance(k, int) and k == SB

    def tiles(k):
        return 1 if is_tail(k) else G

    def cols(table, k):
        return table[:, T:T + 1] if is_tail(k) else table[:, bass.ds(k * G, G)]

    ZW = (N + SPARE) * F // P // 16
    assert ZW * P * 16 == (N + SPARE) * F and ZW >= G * F

    with ExitStack() as ctx:
        def sb(name, shape, dt=F32):
            return ctx.enter_context(nc.sbuf_tensor(name, shape, dt))

        def sem(name):
            return ctx.enter_context(nc.semaphore(name))

        def two(make, name, *args):
            return [make(f"{name}{n}", *args) for n in range(2)]

        def four(make, name, *args):
            return [two(make, f"{name}{c}_", *args) for c in "sd"]

        zeros = sb("zeros", [P, ZW])
        ident = sb("ident", [P, P])
        earlier = sb("earlier", [P, G * P])
        w1 = sb("w1", [2 * F, HID])
        w2 = sb("w2", [HID, F])
        b1c = sb("b1c", [HID, 1])
        b2r = sb("b2r", [P, F])
        wqkv = sb("wqkv", [F, 3 * F])
        eps = sb("eps", [P, 1])
        idx_i = [sb("src_i", [P, T + 1], I32), sb("dst_i", [P, T + 1], I32)]
        idx_f = [sb("src_f", [P, T + 1]), sb("dst_f", [P, T + 1])]
        to_spare = [sb("src_spare", [P, T + 1]), sb("dst_spare", [P, T + 1])]
        spare_i = sb("spare_i", [P, G], I32)
        spare_f = sb("spare_f", [P, G])
        ew = sb("ew", [P, T + 1])
        ew2 = sb("ew2", [P, T + 1])
        weight = sb("weight", [P, T + 1])

        attr = two(sb, "attr", [P, G * F])
        col = four(sb, "col", [P, G])
        same = four(sb, "same", [P, G * G * P])
        rank = four(sb, "rank", [P, G])
        move = four(sb, "move", [P, G])
        target = four(sb, "target", [P, G], I32)
        pay = four(sb, "pay", [P, G * F])
        gidx = two(sb, "gidx", [P, G], I32)
        xg = two(sb, "xg", [P, G * F])
        xgT = two(sb, "xgT", [F, G * P])
        k_sb = two(sb, "k_sb", [P, G * F])
        qk = two(sb, "qk", [P, G * F])
        alpha = two(sb, "alpha", [P, G * HEADS])
        alpha_w = two(sb, "alpha_w", [P, G * HEADS])
        msg = two(sb, "msg", [P, G * F])

        x_in = two(sb, "x_in", [P, CF])
        as_in = two(sb, "as_in", [P, CF])
        ad_in = two(sb, "ad_in", [P, CF])
        xa = two(sb, "xa", [P, C * 2 * F])
        xb = two(sb, "xb", [P, CF])
        xaT = two(sb, "xaT", [2 * F, 4 * P])
        hT = two(sb, "hT", [HID, 4 * P])
        res = two(sb, "res", [P, CF])
        dev = two(sb, "dev", [P, CF])
        sq = two(sb, "sq", [P, CF])
        total = two(sb, "total", [P, C])
        sqsum = two(sb, "sqsum", [P, C])
        std = two(sb, "std", [P, C])
        rstd = two(sb, "rstd", [P, C])
        y_out = two(sb, "y_out", [P, CF])

        pairs = [ctx.enter_context(nc.psum_tensor(f"pair{b}", [P, 1024], F32)) for b in range(4)]
        banks = [pairs[b // 2][:, b % 2 * 512:b % 2 * 512 + 512] for b in range(8)]
        row_ps = [[banks[0], banks[1]], [banks[2], banks[3]]]
        sum_ps = [[banks[4], banks[5]], [banks[6], banks[7]]]
        QKV = 256
        qkv_ps = [pairs[1][:, 0:G * QKV].rearrange("p (g f) -> p g f", f=QKV),
                  pairs[3][:, 0:G * QKV].rearrange("p (g f) -> p g f", f=QKV)]
        xgT_ps = [pairs[1][0:F, 0:G * P], pairs[3][0:F, 0:G * P]]
        xaT_ps = banks[0:2]
        h_ps = banks[2:4]
        y_ps = [banks[4:6], banks[6:8]]
        HALF = C // 2

        S = {name: sem(name) for name in (
            "zero_made zeroed dense_consts idx_loaded filled ident_made mask_made spare_made table_step tables_made "
            "wqkv_zero wqkv_loaded eps_made "
            "a_x_copied a_prepped a_turned a_turn_sb a_h a_h_sb a_y a_res a_sum a_dev a_sq a_sqsum a_std a_rstd a_out "
            "m_gidx m_asked m_turned m_turn_sb m_qkv m_k_sb m_qk m_alpha m_alpha_w m_msg "
            "f_sum f_dev f_sq f_sqsum f_std f_rstd f_out").split()}
        attr_in = two(sem, "attr_in")
        a_in = two(sem, "a_in")
        a_stored = two(sem, "a_stored")
        m_got = two(sem, "m_got")
        f_in = two(sem, "f_in")
        f_stored = two(sem, "f_stored")
        chain = [{n: sem(f"{n}_{c}") for n in
                  ("col", "row", "same", "moved", "target", "sum", "pay", "scatter", "landed")}
                 for c in ("s1", "d1", "s2")]

        block = ctx.enter_context(nc.Block())

        def at(i, off):
            return 2 * i + off, off % 2, i + off // 2

        def exists(step, last):
            return not isinstance(step, int) or 0 <= step <= last

        def reuse(eng, semaphore, count):
            if not isinstance(count, int) or count > 0:
                eng.wait_ge(semaphore, count)

        def v3(tile, n, inner=F):
            return tile.rearrange("p (c f) -> p c f", f=inner)

        @block.sync
        def _(sp):
            for c, idx in enumerate((src, dst)):
                sp.dma_start(idx_i[c][:, 0:T], idx[0:P * T].rearrange("(p t) -> p t", p=P)).then_inc(S["idx_loaded"], 16)
                sp.dma_start(idx_i[c][0:TAIL, T:T + 1],
                             idx[P * T:E].rearrange("(p t) -> p t", p=TAIL)).then_inc(S["idx_loaded"], 16)
            for tile, w in ((ew, edge_w), (ew2, edge_w2)):
                sp.dma_start(tile[:, 0:T], w[0:P * T].rearrange("(p t) -> p t", p=P)).then_inc(S["idx_loaded"], 16)
                sp.dma_start(tile[0:TAIL, T:T + 1],
                             w[P * T:E].rearrange("(p t) -> p t", p=TAIL)).then_inc(S["idx_loaded"], 16)
            sp.wait_ge(S["zero_made"], 1)
            for a in agg:
                sp.dma_start(a.rearrange("n f -> (n f)").rearrange("(p r w) -> p r w", p=P, r=16),
                             zeros[:, :].unsqueeze(1).to_broadcast([P, 16, ZW])).then_inc(S["zeroed"], 16)
            sp.dma_start(acc[N:N + SPARE, :].rearrange("(p g) f -> p (g f)", p=P),
                         zeros[:, 0:G * F]).then_inc(S["zeroed"], 16)
            sp.dma_start(w1[:, :], W1).then_inc(S["dense_consts"], 16)
            sp.dma_start(w2[:, :], W2).then_inc(S["dense_consts"], 16)
            sp.dma_start(b1c[:, :], b1.rearrange("(h o) -> h o", o=1)).then_inc(S["dense_consts"], 16)
            sp.dma_start(b2r[:, :], b2.rearrange("(o f) -> o f", o=1).to_broadcast([P, F])).then_inc(S["dense_consts"], 16)
            sp.wait_ge(S["wqkv_zero"], 1)
            for n, w in enumerate((Wq, Wk, Wv)):
                for h in range(HEADS):
                    sp.dma_start(wqkv[h * FH:(h + 1) * FH, n * F + h * FH:n * F + (h + 1) * FH],
                                 w[h]).then_inc(S["wqkv_loaded"], 16)

            attr_main = edge_attr[0:P * T, :].rearrange("(p t) f -> p (t f)", p=P)

            def load_attr(i, off):
                k, s, _ = at(i, off)
                for c in (0, 1):
                    reuse(sp, chain[c]["sum"], k - 1)
                if is_tail(k):
                    sp.dma_start(attr[s][0:TAIL, 0:F], edge_attr[P * T:E, :]).then_inc(attr_in[s], 16)
                else:
                    sp.dma_start(attr[s][:, :], attr_main[:, bass.ds(k * G * F, G * F)]).then_inc(attr_in[s], 16)

            for n in range(4):
                load_attr(0, n)
            with sp.Fori(2, SB // 2) as i:
                load_attr(i, 0)
                load_attr(i, 1)
            load_attr(0, SB)

            sp.wait_ge(chain[0]["scatter"], 16 * (T + 1))
            sp.wait_ge(chain[1]["scatter"], 16 * (T + 1))

            def load_nodes(i, off):
                q, s, _ = at(i, off)
                reuse(sp, S["a_x_copied"], q - 1)
                reuse(sp, S["a_prepped"], q - 1)
                for tile, a in ((x_in, x), (as_in, agg_src), (ad_in, agg_dst)):
                    sp.dma_start(tile[s][0:rows(q), :], chunk_of(a, q)).then_inc(a_in[s], 16)

            for n in range(4):
                load_nodes(0, n)
            with sp.Fori(2, CHUNKS // 2) as i:
                load_nodes(i, 0)
                load_nodes(i, 1)
            load_nodes(0, CHUNKS)

            sp.wait_ge(chain[2]["scatter"], 16 * (T + 1))

            def load_acc(i, off):
                q, s, _ = at(i, off)
                reuse(sp, S["f_dev"], q - 1)
                sp.dma_start(x_in[s][0:rows(q), :], chunk_of(acc, q)).then_inc(f_in[s], 16)

            for n in range(4):
                load_acc(0, n)
            with sp.Fori(2, CHUNKS // 2) as i:
                load_acc(i, 0)
                load_acc(i, 1)
            load_acc(0, CHUNKS)
            sp.wait_ge(f_stored[0], 16 * (CHUNKS // 2 + 1))
            sp.wait_ge(f_stored[1], 16 * (CHUNKS // 2))

        @block.gpsimd
        def _(pool):
            nc.gpsimd.memset(ident[:, :], 0.0).then_inc(S["filled"], 1)
            nc.gpsimd.memset(earlier[:, :], 1.0).then_inc(S["filled"], 1)
            pool.wait_ge(S["filled"], 2)
            nc.gpsimd.affine_select(out=ident[:, :], in_=ident[:, :], compare_op=ALU.not_equal, fill=1.0, base=0,
                                    pattern=[[-1, P]], channel_multiplier=1).then_inc(S["ident_made"], 1)
            own = earlier[:, (G - 1) * P:G * P]
            nc.gpsimd.affine_select(out=own, in_=own, compare_op=ALU.is_ge, fill=0.0, base=0,
                                    pattern=[[-1, P]], channel_multiplier=1).then_inc(S["mask_made"], 1)
            nc.gpsimd.iota(spare_i[:, :], pattern=[[P, G]], base=N, channel_multiplier=1).then_inc(S["spare_made"], 1)

            def scatter(ch, dest, c, i, off):
                k, s, _ = at(i, off)
                sm = chain[ch]
                pool.wait_ge(sm["target"], k + 1)
                pool.wait_ge(sm["pay"], k + 1)
                if not isinstance(k, int) or k > 0:
                    pool.wait_ge(sm["scatter"], 16 * G * k)
                    pool.sem_inc(sm["landed"], 1)
                for g in range(tiles(k)):
                    nc.gpsimd.indirect_dma_start(
                        dest[:, :], bass.IndirectOffsetOnAxis(ap=target[c][s][:, g:g + 1], axis=0),
                        pay[c][s][:, g * F:(g + 1) * F], None, compute_op=ALU.add).then_inc(sm["scatter"], 16)

            def sums_step(i, off):
                for c in (0, 1):
                    scatter(c, agg[c], c, i, off)

            pool.wait_ge(S["zeroed"], 48)
            for n in range(4):
                sums_step(0, n)
            with pool.Fori(2, SB // 2) as i:
                sums_step(i, 0)
                sums_step(i, 1)
            sums_step(0, SB)

            def prep(i, off):
                q, s, m = at(i, off)
                n = rows(q)
                pool.wait_ge(a_in[s], 48 * (m + 1))
                reuse(pool, S["a_turned"], 3 * (q - 1))
                nc.gpsimd.tensor_tensor(xa[s][0:n, :].rearrange("p (c f) -> p c f", c=C)[:, :, F:2 * F],
                                        v3(as_in[s][0:n, :], n), v3(ad_in[s][0:n, :], n), ALU.add)
                reuse(pool, S["a_res"], q - 1)
                nc.gpsimd.tensor_tensor(v3(xb[s][0:n, :], n), v3(x_in[s][0:n, :], n),
                                        b2r[0:n, :].unsqueeze(1).to_broadcast([n, C, F]),
                                        ALU.add).then_inc(S["a_prepped"], 1)

            def scale(pre, stored, per_store, i, off):
                q, s, m = at(i, off)
                n = rows(q)
                pool.wait_ge(S[pre + "rstd"], q + 1)
                reuse(pool, stored[s], per_store * m)
                nc.gpsimd.tensor_tensor(v3(y_out[s][0:n, :], n), v3(dev[s][0:n, :], n),
                                        rstd[s][0:n, :].unsqueeze(2).to_broadcast([n, C, F]),
                                        ALU.mult).then_inc(S[pre + "out"], 1)

            def dense_step(i, off):
                if exists(at(i, off)[0], CHUNKS):
                    prep(i, off)
                if exists(at(i, off - 3)[0], CHUNKS):
                    scale("a_", a_stored, 32, i, off - 3)

            pool.wait_ge(S["dense_consts"], 64)
            for n in range(6):
                dense_step(0, n)
            with pool.Fori(3, CHUNKS // 2) as i:
                dense_step(i, 0)
                dense_step(i, 1)
            for q in range(CHUNKS, CHUNKS + 4):
                dense_step(0, q)

            def gather(i, off):
                k, s, m = at(i, off)
                pool.wait_ge(S["m_gidx"], k + 1)
                reuse(pool, S["m_turned"], k - 1)
                pool.sem_inc(S["m_asked"], 1)
                n = TAIL if is_tail(k) else P
                for g in range(tiles(k)):
                    nc.gpsimd.indirect_dma_start(
                        xg[s][0:n, g * F:(g + 1) * F], None, x1[:, :],
                        bass.IndirectOffsetOnAxis(ap=gidx[s][0:n, g:g + 1], axis=0)).then_inc(m_got[s], 16)

            def attend_step(i, off):
                if exists(at(i, off)[0], SB):
                    gather(i, off)
                if exists(at(i, off - 2)[0], SB):
                    scatter(2, acc, 0, i, off - 2)

            pool.wait_ge(a_stored[0], 32 * (CHUNKS // 2 + 1))
            pool.wait_ge(a_stored[1], 32 * (CHUNKS // 2))
            for n in range(4):
                attend_step(0, n)
            with pool.Fori(2, SB // 2) as i:
                attend_step(i, 0)
                attend_step(i, 1)
            for k in range(SB, SB + 3):
                attend_step(0, k)

            def last_step(i, off):
                if exists(at(i, off - 2)[0], CHUNKS):
                    scale("f_", f_stored, 16, i, off - 2)

            last_step(0, 2)
            last_step(0, 3)
            with pool.Fori(2, CHUNKS // 2) as i:
                last_step(i, 0)
                last_step(i, 1)
            for q in range(CHUNKS, CHUNKS + 3):
                last_step(0, q)

        @block.scalar
        def _(act):
            def stage_col(ch, c, i, off):
                k, s, _ = at(i, off)
                reuse(act, chain[ch]["target"], k - 1)
                nc.scalar.copy(col[c][s][:, 0:tiles(k)], cols(idx_f[c], k)).then_inc(chain[ch]["col"], 1)

            def copy_pay(ch, c, i, off):
                k, s, _ = at(i, off)
                act.wait_ge(chain[ch]["sum"], k + 1)
                reuse(act, chain[ch]["landed"], k - 1)
                w = tiles(k) * F
                nc.scalar.copy(pay[c][s][:, 0:w], sum_ps[c][s][:, 0:w]).then_inc(chain[ch]["pay"], 1)

            def sums_step(i, off):
                for c in (0, 1):
                    if exists(at(i, off)[0], SB):
                        stage_col(c, c, i, off)
                for c in (0, 1):
                    if exists(at(i, off - 1)[0], SB):
                        copy_pay(c, c, i, off - 1)

            act.wait_ge(S["tables_made"], 1)
            for n in range(4):
                sums_step(0, n)
            with act.Fori(2, SB // 2) as i:
                sums_step(i, 0)
                sums_step(i, 1)
            sums_step(0, SB)
            sums_step(0, SB + 1)

            def copy_x(i, off):
                q, s, m = at(i, off)
                n = rows(q)
                act.wait_ge(a_in[s], 48 * (m + 1))
                reuse(act, S["a_turned"], 3 * (q - 1))
                nc.scalar.copy(xa[s][0:n, :].rearrange("p (c f) -> p c f", c=C)[:, :, 0:F],
                               v3(x_in[s][0:n, :], n)).then_inc(S["a_x_copied"], 1)

            def copy_turned(i, n3):
                q, g, u = 2 * i + n3 // 3, n3 % 3, n3 % 2
                w = GROUPS[g][1] * rows(q)
                act.wait_ge(S["a_turned"], 3 * q + g + 1)
                reuse(act, S["a_h"], 3 * q + g - 1)
                nc.scalar.copy(xaT[u][:, 0:w], xaT_ps[u][:, 0:w]).then_inc(S["a_turn_sb"], 1)

            def relu(i, n3):
                q, g, u = 2 * i + n3 // 3, n3 % 3, n3 % 2
                if not exists(q, CHUNKS):
                    return
                w = GROUPS[g][1] * rows(q)
                act.wait_ge(S["a_h"], 3 * q + g + 1)
                reuse(act, S["a_y"], 3 * q + g - 1)
                nc.scalar.activation(hT[u][:, 0:w], h_ps[u][:, 0:w], ACT.Relu,
                                     bias=b1c[:, 0:1]).then_inc(S["a_h_sb"], 1)

            def square(pre, i, off):
                q, s, _ = at(i, off)
                if not exists(q, CHUNKS):
                    return
                n = rows(q)
                act.wait_ge(S[pre + "dev"], q + 1)
                reuse(act, S[pre + "sqsum"], q - 1)
                nc.scalar.activation(sq[s][0:n, :], dev[s][0:n, :], ACT.Square).then_inc(S[pre + "sq"], 1)

            def root(pre, i, off):
                q, s, _ = at(i, off)
                if not exists(q, CHUNKS):
                    return
                n = rows(q)
                act.wait_ge(S[pre + "sqsum"], q + 1)
                reuse(act, S[pre + "rstd"], q - 1)
                nc.scalar.activation(std[s][0:n, :], sqsum[s][0:n, :], ACT.Sqrt, scale=1.0 / F,
                                     bias=eps[0:n, 0:1]).then_inc(S[pre + "std"], 1)

            def store(pre, dests, stored, i, off):
                q, s, _ = at(i, off)
                if not exists(q, CHUNKS):
                    return
                act.wait_ge(S[pre + "out"], q + 1)
                for dest in dests:
                    act.dma_start(chunk_of(dest, q), y_out[s][0:rows(q), :]).then_inc(stored[s], 16)

            def dense_step(i, off):
                here = exists(at(i, off)[0], CHUNKS)
                if here:
                    copy_x(i, off)
                for g in range(3):
                    if here:
                        copy_turned(i, 3 * off + g)
                    relu(i, 3 * off + g - 1)
                    if g == 0:
                        square("a_", i, off - 2)
                root("a_", i, off - 2)
                store("a_", (x1, acc), a_stored, i, off - 3)

            act.wait_ge(S["dense_consts"], 64)
            act.wait_ge(S["eps_made"], 1)
            for n in range(4):
                dense_step(0, n)
            with act.Fori(2, CHUNKS // 2) as i:
                dense_step(i, 0)
                dense_step(i, 1)
            for q in range(CHUNKS, CHUNKS + 4):
                dense_step(0, q)

            def stage_gather(i, off):
                k, s, m = at(i, off)
                reuse(act, m_got[s], 16 * G * m)
                nc.scalar.copy(gidx[s][:, 0:tiles(k)], cols(idx_f[1], k)).then_inc(S["m_gidx"], 1)

            def copy_edges(i, off):
                k, s, _ = at(i, off)
                w = tiles(k)
                act.wait_ge(S["m_turned"], k + 1)
                reuse(act, S["m_qkv"], k - 1)
                nc.scalar.copy(xgT[s][:, 0:w * P], xgT_ps[s][:, 0:w * P]).then_inc(S["m_turn_sb"], 1)
                act.wait_ge(S["m_qkv"], k + 1)
                reuse(act, S["m_qk"], k - 1)
                nc.scalar.copy(v3(k_sb[s][:, 0:w * F], P), qkv_ps[s][:, 0:w, F:2 * F]).then_inc(S["m_k_sb"], 1)

            def attend_step(i, off):
                if exists(at(i, off)[0], SB):
                    stage_col(2, 0, i, off)
                if exists(at(i, off + 1)[0], SB):
                    stage_gather(i, off + 1)
                if exists(at(i, off)[0], SB):
                    copy_edges(i, off)
                if exists(at(i, off - 1)[0], SB):
                    copy_pay(2, 0, i, off - 1)

            stage_gather(0, 0)
            for n in range(4):
                attend_step(0, n)
            with act.Fori(2, SB // 2 - 1) as i:
                attend_step(i, 0)
                attend_step(i, 1)
            for k in range(SB - 2, SB + 2):
                attend_step(0, k)

            def last_step(i, off):
                root("f_", i, off - 1)
                square("f_", i, off)
                store("f_", (out,), f_stored, i, off - 2)

            for n in range(4):
                last_step(0, n)
            with act.Fori(2, CHUNKS // 2) as i:
                last_step(i, 0)
                last_step(i, 1)
            for q in range(CHUNKS, CHUNKS + 3):
                last_step(0, q)

        @block.tensor
        def _(pe):
            def turn_cols(ch, c, i, off):
                k, s, _ = at(i, off)
                pe.wait_ge(chain[ch]["col"], k + 1)
                reuse(pe, chain[ch]["same"], k - 1)
                for g in range(tiles(k)):
                    last = nc.tensor.transpose(row_ps[c][s][:, g * P:(g + 1) * P],
                                               col[c][s][:, g:g + 1].to_broadcast([P, P]), ident[:, :])
                last.then_inc(chain[ch]["row"], 1)

            def sum_same(ch, c, rows_of, i, off):
                k, s, _ = at(i, off)
                pe.wait_ge(chain[ch]["same"], k + 1)
                reuse(pe, chain[ch]["pay"], k - 1)
                for a in range(tiles(k)):
                    for b in range(a, tiles(k)):
                        at_b = b * G * P + a * P
                        last = nc.tensor.matmul(sum_ps[c][s][:, a * F:(a + 1) * F], same[c][s][:, at_b:at_b + P],
                                                rows_of[s][:, b * F:(b + 1) * F],
                                                start=(b == a), stop=(b == tiles(k) - 1))
                last.then_inc(chain[ch]["sum"], 1)

            def sums_step(i, off):
                for c in (0, 1):
                    if exists(at(i, off)[0], SB):
                        turn_cols(c, c, i, off)
                if exists(at(i, off - 1)[0], SB):
                    _, s, m = at(i, off - 1)
                    pe.wait_ge(attr_in[s], 16 * (m + 1))
                    for c in (0, 1):
                        sum_same(c, c, attr, i, off - 1)

            pe.wait_ge(S["ident_made"], 1)
            for n in range(4):
                sums_step(0, n)
            with pe.Fori(2, SB // 2) as i:
                sums_step(i, 0)
                sums_step(i, 1)
            sums_step(0, SB)
            sums_step(0, SB + 1)

            def turn_nodes(i, n3):
                q, g, u = 2 * i + n3 // 3, n3 % 3, n3 % 2
                if not exists(q, CHUNKS):
                    return
                s, n = (n3 // 3) % 2, rows(q)
                if g == 0:
                    pe.wait_ge(S["a_x_copied"], q + 1)
                    pe.wait_ge(S["a_prepped"], q + 1)
                reuse(pe, S["a_turn_sb"], 3 * q + g - 1)
                c0, nc_ = GROUPS[g]
                for c in range(nc_):
                    last = nc.tensor.transpose(xaT_ps[u][:, c * n:(c + 1) * n],
                                               xa[s][0:n, (c0 + c) * 2 * F:(c0 + c + 1) * 2 * F], ident[0:n, 0:n])
                last.then_inc(S["a_turned"], 1)

            def hidden(i, n3):
                q, g, u = 2 * i + n3 // 3, n3 % 3, n3 % 2
                if not exists(q, CHUNKS):
                    return
                w = GROUPS[g][1] * rows(q)
                pe.wait_ge(S["a_turn_sb"], 3 * q + g + 1)
                reuse(pe, S["a_h_sb"], 3 * q + g - 1)
                nc.tensor.matmul(h_ps[u][:, 0:w], w1[:, :], xaT[u][:, 0:w], start=True,
                                 stop=True).then_inc(S["a_h"], 1)

            def project(i, n3):
                q, g, u = 2 * i + n3 // 3, n3 % 3, n3 % 2
                if not exists(q, CHUNKS):
                    return
                s, n = (n3 // 3) % 2, rows(q)
                pe.wait_ge(S["a_h_sb"], 3 * q + g + 1)
                if g == 0:
                    reuse(pe, S["a_res"], q - 1)
                c0, nc_ = GROUPS[g]
                for c in range(nc_):
                    half, at_c = (c0 + c) // HALF, (c0 + c) % HALF * F
                    last = nc.tensor.matmul(y_ps[s][half][0:n, at_c:at_c + F], hT[u][:, c * n:(c + 1) * n],
                                            w2[:, :], start=True, stop=True)
                last.then_inc(S["a_y"], 1)

            def dense_step(i, off):
                for g in range(3):
                    turn_nodes(i, 3 * off + g)
                    hidden(i, 3 * off + g - 1)
                    project(i, 3 * off + g - 2)

            pe.wait_ge(S["dense_consts"], 64)
            for n in range(4):
                dense_step(0, n)
            with pe.Fori(2, CHUNKS // 2) as i:
                dense_step(i, 0)
                dense_step(i, 1)
            dense_step(0, CHUNKS)
            dense_step(0, CHUNKS + 1)

            def project_edges(i, off):
                k, s, m = at(i, off)
                for g in range(tiles(k)):
                    last = nc.tensor.transpose(xgT_ps[s][:, g * P:(g + 1) * P], xg[s][:, g * F:(g + 1) * F],
                                               ident[:, :])
                last.then_inc(S["m_turned"], 1)
                pe.wait_ge(S["m_turn_sb"], k + 1)
                for g in range(tiles(k)):
                    last = nc.tensor.matmul(qkv_ps[s][:, g, 0:3 * F], xgT[s][:, g * P:(g + 1) * P], wqkv[:, :],
                                            start=True, stop=True)
                last.then_inc(S["m_qkv"], 1)

            def attend_step(i, off):
                k, s, m = at(i, off)
                if exists(k, SB):
                    pe.wait_ge(m_got[s], 16 * G * m + 16 * tiles(k))
                    reuse(pe, S["m_msg"], k - 1)
                    turn_cols(2, 0, i, off)
                    project_edges(i, off)
                if exists(at(i, off - 1)[0], SB):
                    pe.wait_ge(S["m_msg"], at(i, off - 1)[0] + 1)
                    sum_same(2, 0, msg, i, off - 1)

            pe.wait_ge(S["wqkv_loaded"], 16 * 3 * HEADS)
            for n in range(4):
                attend_step(0, n)
            with pe.Fori(2, SB // 2) as i:
                attend_step(i, 0)
                attend_step(i, 1)
            attend_step(0, SB)
            attend_step(0, SB + 1)

        @block.vector
        def _(dve):
            nc.vector.memset(zeros[:, :], 0.0).then_inc(S["zero_made"], 1)
            nc.vector.memset(wqkv[:, :], 0.0).then_inc(S["wqkv_zero"], 1)
            nc.vector.memset(eps[:, :], EPS).then_inc(S["eps_made"], 1)
            nc.vector.memset(weight[:, T:T + 1], 0.0)
            dve.wait_ge(S["spare_made"], 1)
            nc.vector.tensor_copy(spare_f[:, :], spare_i[:, :]).then_inc(S["table_step"], 1)
            dve.wait_ge(S["table_step"], 1)
            dve.wait_ge(S["idx_loaded"], 16 * 8)
            for c in (0, 1):
                nc.vector.tensor_copy(idx_f[c][:, 0:T], idx_i[c][:, 0:T])
                nc.vector.tensor_copy(idx_f[c][:, T:T + 1], spare_f[:, 0:1]).then_inc(S["table_step"], 1)
            dve.wait_ge(S["table_step"], 3)
            for c in (0, 1):
                nc.vector.tensor_copy(idx_f[c][0:TAIL, T:T + 1], idx_i[c][0:TAIL, T:T + 1]).then_inc(S["table_step"], 1)
            for n, lo, hi in ((P, 0, T), (TAIL, T, T + 1)):
                nc.vector.scalar_tensor_tensor(out=weight[0:n, lo:hi], in0=ew[0:n, lo:hi], scalar=float(FH) ** -0.5,
                                               in1=ew2[0:n, lo:hi], op0=ALU.mult, op1=ALU.mult)
            dve.wait_ge(S["table_step"], 5)
            for c in (0, 1):
                nc.vector.tensor_tensor(to_spare[c][:, 0:T].rearrange("p (k g) -> p k g", g=G),
                                        spare_f[:, :].unsqueeze(1).to_broadcast([P, SB, G]),
                                        idx_f[c][:, 0:T].rearrange("p (k g) -> p k g", g=G), ALU.subtract)
                last = nc.vector.tensor_tensor(to_spare[c][:, T:T + 1], spare_f[:, 0:1], idx_f[c][:, T:T + 1],
                                               ALU.subtract)
            last.then_inc(S["tables_made"], 1)
            dve.wait_ge(S["tables_made"], 1)
            dve.wait_ge(S["mask_made"], 1)

            def compare(ch, c, i, off):
                k, s, _ = at(i, off)
                sm, t = chain[ch], tiles(k)
                dve.wait_ge(sm["row"], k + 1)
                reuse(dve, sm["sum"], k - 1)
                for b in range(t):
                    w = (b + 1) * P
                    last = nc.vector.scalar_tensor_tensor(
                        out=same[c][s][:, b * G * P:b * G * P + w], in0=row_ps[c][s][:, 0:w],
                        scalar=col[c][s][:, b:b + 1], in1=earlier[:, G * P - w:G * P],
                        op0=ALU.is_equal, op1=ALU.mult, accum_out=rank[c][s][:, b:b + 1])
                last.then_inc(sm["same"], 1)
                dve.wait_ge(sm["same"], k + 1)
                nc.vector.scalar_tensor_tensor(out=move[c][s][:, 0:t], in0=rank[c][s][:, 0:t], scalar=1.5,
                                               in1=cols(to_spare[c], k), op0=ALU.is_gt,
                                               op1=ALU.mult).then_inc(sm["moved"], 1)
                dve.wait_ge(sm["moved"], k + 1)
                reuse(dve, sm["landed"], k - 1)
                nc.vector.tensor_tensor(target[c][s][:, 0:t], move[c][s][:, 0:t], col[c][s][:, 0:t],
                                        ALU.add).then_inc(sm["target"], 1)

            def sums_step(i, off):
                for c in (0, 1):
                    compare(c, c, i, off)

            for n in range(4):
                sums_step(0, n)
            with dve.Fori(2, SB // 2) as i:
                sums_step(i, 0)
                sums_step(i, 1)
            sums_step(0, SB)

            def deviate(pre, value, i, off):
                q, s, _ = at(i, off)
                n = rows(q)
                nc.vector.tensor_reduce(total[s][0:n, :], v3(value[s][0:n, :], n), AX_X,
                                        ALU.add).then_inc(S[pre + "sum"], 1)
                dve.wait_ge(S[pre + "sum"], q + 1)
                reuse(dve, S[pre + "out"], q - 1)
                nc.vector.scalar_tensor_tensor(out=v3(dev[s][0:n, :], n),
                                               in0=total[s][0:n, :].unsqueeze(2).to_broadcast([n, C, F]),
                                               scalar=-1.0 / F, in1=v3(value[s][0:n, :], n), op0=ALU.mult,
                                               op1=ALU.add).then_inc(S[pre + "dev"], 1)

            def sum_squares(pre, i, off):
                q, s, _ = at(i, off)
                if not exists(q, CHUNKS):
                    return
                n = rows(q)
                dve.wait_ge(S[pre + "sq"], q + 1)
                nc.vector.tensor_reduce(sqsum[s][0:n, :], v3(sq[s][0:n, :], n), AX_X,
                                        ALU.add).then_inc(S[pre + "sqsum"], 1)

            def invert(pre, i, off):
                q, s, _ = at(i, off)
                if not exists(q, CHUNKS):
                    return
                n = rows(q)
                dve.wait_ge(S[pre + "std"], q + 1)
                nc.vector.reciprocal(rstd[s][0:n, :], std[s][0:n, :]).then_inc(S[pre + "rstd"], 1)

            def dense_step(i, off):
                sum_squares("a_", i, off - 1)
                q, s, _ = at(i, off)
                if exists(q, CHUNKS):
                    n = rows(q)
                    dve.wait_ge(S["a_prepped"], q + 1)
                    dve.wait_ge(S["a_y"], 3 * q + 3)
                    for half in (0, 1):
                        lo = half * HALF * F
                        last = nc.vector.tensor_tensor(res[s][0:n, lo:lo + HALF * F], y_ps[s][half][0:n, 0:HALF * F],
                                                       xb[s][0:n, lo:lo + HALF * F], ALU.add)
                    last.then_inc(S["a_res"], 1)
                    dve.wait_ge(S["a_res"], q + 1)
                    deviate("a_", res, i, off)
                invert("a_", i, off - 1)

            for n in range(4):
                dense_step(0, n)
            with dve.Fori(2, CHUNKS // 2) as i:
                dense_step(i, 0)
                dense_step(i, 1)
            dense_step(0, CHUNKS)
            dense_step(0, CHUNKS + 1)

            def message(i, off):
                k, s, _ = at(i, off)
                t = tiles(k)
                dve.wait_ge(S["m_k_sb"], k + 1)
                nc.vector.tensor_tensor(v3(qk[s][:, 0:t * F], P),
                                        qkv_ps[s][:, 0:t, 0:F],
                                        v3(k_sb[s][:, 0:t * F], P), ALU.mult).then_inc(S["m_qk"], 1)
                dve.wait_ge(S["m_qk"], k + 1)
                nc.vector.tensor_reduce(alpha[s][:, 0:t * HEADS],
                                        qk[s][:, 0:t * F].rearrange("p (h f) -> p h f", f=FH), AX_X,
                                        ALU.add).then_inc(S["m_alpha"], 1)
                dve.wait_ge(S["m_alpha"], k + 1)
                nc.vector.tensor_tensor(alpha_w[s][:, 0:t * HEADS].rearrange("p (g h) -> p g h", h=HEADS),
                                        alpha[s][:, 0:t * HEADS].rearrange("p (g h) -> p g h", h=HEADS),
                                        cols(weight, k).unsqueeze(2).to_broadcast([P, t, HEADS]),
                                        ALU.mult).then_inc(S["m_alpha_w"], 1)
                dve.wait_ge(S["m_alpha_w"], k + 1)
                nc.vector.tensor_tensor(msg[s][:, 0:t * F].rearrange("p (g h f) -> p g h f", g=t, f=FH),
                                        qkv_ps[s][:, 0:t, 2 * F:3 * F].rearrange("p g (h f) -> p g h f", f=FH),
                                        alpha_w[s][:, 0:t * HEADS].rearrange("p (g h) -> p g h", h=HEADS)
                                        .unsqueeze(3).to_broadcast([P, t, HEADS, FH]),
                                        ALU.mult).then_inc(S["m_msg"], 1)

            def attend_step(i, off):
                compare(2, 0, i, off)
                message(i, off)

            for n in range(4):
                attend_step(0, n)
            with dve.Fori(2, SB // 2) as i:
                attend_step(i, 0)
                attend_step(i, 1)
            attend_step(0, SB)

            def last_step(i, off):
                q, s, m = at(i, off)
                sum_squares("f_", i, off - 1)
                if exists(q, CHUNKS):
                    dve.wait_ge(f_in[s], 16 * (m + 1))
                    deviate("f_", x_in, i, off)
                invert("f_", i, off - 1)

            for n in range(4):
                last_step(0, n)
            with dve.Fori(2, CHUNKS // 2) as i:
                last_step(i, 0)
                last_step(i, 1)
            for q in range(CHUNKS, CHUNKS + 3):
                last_step(0, q)


_INS = ["x", "src", "dst", "edge_attr_64", "edge_weight", "edge_weight_n2", "L0_gnn_W1", "L0_gnn_b1", "L0_gnn_W2",
        "L0_gnn_b2", "L1_gnn_Wq", "L1_gnn_Wk", "L1_gnn_Wv"]


def kernel(**inputs):
    import numpy as _np
    import concourse.bacc as _bacc
    from concourse import mybir as _mybir
    from concourse.bass_utils import run_bass_kernel_spmd as _run

    nc = _bacc.Bacc("TRN2", target_bir_lowering=False, num_devices=1)
    arrays, args = {}, []
    for name in _INS:
        a = _np.ascontiguousarray(inputs[name])
        arrays[f"in_{name}"] = a
        args.append(nc.dram_tensor(f"in_{name}", a.shape, _mybir.dt.from_np(a.dtype), kind="ExternalInput").ap())
    out = nc.dram_tensor("out_0", inputs["x"].shape, _mybir.dt.float32, kind="ExternalOutput").ap()
    build(nc, *args, out)
    r = _run(nc, [arrays], core_ids=[0])
    return r.results[0]["out_0"]
```

```python
from contextlib import ExitStack

import concourse.bass as bass
from concourse import mybir

F32 = mybir.dt.float32
I32 = mybir.dt.int32
ALU = mybir.AluOpType
ACT = mybir.ActivationFunctionType
AX_X = mybir.AxisListType.X

P = 128
G = 4
C = 10
GROUPS = [(0, 4), (4, 4), (8, 2)]
EPS = 1e-5


def build(nc, x, src, dst, edge_attr, edge_w, edge_w2, W1, b1, W2, b2, Wq, Wk, Wv, out):
    N, F = x.shape
    E = edge_attr.shape[0]
    HID = W1.shape[1]
    HEADS, FH, _ = Wq.shape

    SB = E // P // G
    T = SB * G
    TF = E // P - T
    TL = T + TF
    TAIL = E - P * TL
    assert 0 < TF < G and 0 < TAIL < P
    CHUNKS = N // P // (2 * C) * 2
    COLS = CHUNKS * C
    REST = (N - P * COLS) // C
    assert REST * C == N - P * COLS and 0 < REST <= 32 and CHUNKS % 4 == 2
    SPARE = G * P
    CF = C * F

    agg_src = nc.dram_tensor("agg_src", (N + SPARE, F), F32).ap()
    agg_dst = nc.dram_tensor("agg_dst", (N + SPARE, F), F32).ap()
    agg = [agg_src, agg_dst]
    x1 = nc.dram_tensor("x1", (N, F), F32).ap()
    acc = nc.dram_tensor("acc", (N + SPARE, F), F32).ap()

    def main_nodes(a):
        return a[0:P * COLS, :].rearrange("(p j) f -> p (j f)", p=P)

    def rest_nodes(a):
        return a[P * COLS:N, :].rearrange("(p j) f -> p (j f)", p=REST)

    def is_rest(q):
        return isinstance(q, int) and q == CHUNKS

    def rows(q):
        return REST if is_rest(q) else P

    def chunk_of(a, q):
        return rest_nodes(a) if is_rest(q) else main_nodes(a)[:, bass.ds(q * CF, CF)]

    def is_tail(k):
        return isinstance(k, int) and k == SB

    def tiles(k):
        return TF + 1 if is_tail(k) else G

    def cols(table, k):
        return table[:, T:TL + 1] if is_tail(k) else table[:, bass.ds(k * G, G)]

    ZR = 16
    ZW = (N + SPARE) * F // P // ZR
    assert ZW * P * ZR == (N + SPARE) * F and ZW >= G * F

    with ExitStack() as ctx:
        def sb(name, shape, dt=F32):
            return ctx.enter_context(nc.sbuf_tensor(name, shape, dt))

        def sem(name):
            return ctx.enter_context(nc.semaphore(name))

        def slots_of(make, name, *args, slots=2):
            return [make(f"{name}{n}", *args) for n in range(slots)]

        def for_chains(make, name, *args, slots=2):
            return [slots_of(make, f"{name}{c}_", *args, slots=slots) for c in "sd"]

        zeros = sb("zeros", [P, ZW])
        ident = sb("ident", [P, P])
        earlier = sb("earlier", [P, G * P])
        w1 = sb("w1", [2 * F, HID])
        w2 = sb("w2", [HID, F])
        b1c = sb("b1c", [HID, 1])
        b2r = sb("b2r", [P, F])
        wqkv = sb("wqkv", [F, 3 * F])
        eps = sb("eps", [P, 1])
        idx_i = [sb("src_i", [P, TL + 1], I32), sb("dst_i", [P, TL + 1], I32)]
        idx_f = [sb("src_f", [P, TL + 1]), sb("dst_f", [P, TL + 1])]
        to_spare = [sb("src_spare", [P, TL + 1]), sb("dst_spare", [P, TL + 1])]
        spare_i = sb("spare_i", [P, G], I32)
        spare_f = sb("spare_f", [P, G])
        ew = sb("ew", [P, TL + 1])
        ew2 = sb("ew2", [P, TL + 1])
        weight = sb("weight", [P, TL + 1])

        attr = slots_of(sb, "attr", [P, G * F])
        col = for_chains(sb, "col", [P, G], slots=4)
        same = for_chains(sb, "same", [P, G * G * P])
        rank = for_chains(sb, "rank", [P, G])
        move = for_chains(sb, "move", [P, G], slots=4)
        target = for_chains(sb, "target", [P, G], I32, slots=4)
        pay = for_chains(sb, "pay", [P, G * F], slots=4)
        gidx = slots_of(sb, "gidx", [P, G], I32, slots=4)
        xg = slots_of(sb, "xg", [P, G * F], slots=4)
        xgT = slots_of(sb, "xgT", [F, G * P])
        k_sb = slots_of(sb, "k_sb", [P, G * F])
        qk = slots_of(sb, "qk", [P, G * F])
        alpha = slots_of(sb, "alpha", [P, G * HEADS])
        alpha_w = slots_of(sb, "alpha_w", [P, G * HEADS])
        msg = slots_of(sb, "msg", [P, G * F])

        x_in = slots_of(sb, "x_in", [P, CF], slots=4)
        as_in = slots_of(sb, "as_in", [P, CF], slots=4)
        ad_in = slots_of(sb, "ad_in", [P, CF], slots=4)
        xa = slots_of(sb, "xa", [P, C * 2 * F])
        xb = slots_of(sb, "xb", [P, CF], slots=4)
        xaT = slots_of(sb, "xaT", [2 * F, 4 * P])
        hT = slots_of(sb, "hT", [HID, 4 * P])
        res = slots_of(sb, "res", [P, CF])
        dev = slots_of(sb, "dev", [P, CF])
        sq = slots_of(sb, "sq", [P, CF])
        total = slots_of(sb, "total", [P, C])
        sqsum = slots_of(sb, "sqsum", [P, C])
        std = slots_of(sb, "std", [P, C])
        rstd = slots_of(sb, "rstd", [P, C])
        y_out = slots_of(sb, "y_out", [P, CF], slots=4)

        pairs = [ctx.enter_context(nc.psum_tensor(f"pair{b}", [P, 1024], F32)) for b in range(4)]
        banks = [pairs[b // 2][:, b % 2 * 512:b % 2 * 512 + 512] for b in range(8)]
        row_ps = [[banks[0], banks[1]], [banks[2], banks[3]]]
        sum_ps = [[banks[4], banks[5]], [banks[6], banks[7]]]
        QKV = 256
        qkv_ps = [pairs[1][:, 0:G * QKV].rearrange("p (g f) -> p g f", f=QKV),
                  pairs[3][:, 0:G * QKV].rearrange("p (g f) -> p g f", f=QKV)]
        xgT_ps = [pairs[1][0:F, 0:G * P], pairs[3][0:F, 0:G * P]]
        xaT_ps = banks[0:2]
        h_ps = banks[2:4]
        y_ps = [banks[4:6], banks[6:8]]
        HALF = C // 2

        S = {name: sem(name) for name in (
            "zero_made zeroed dense_consts idx_loaded filled ident_made mask_made spare_made table_step tables_made "
            "wqkv_zero wqkv_loaded eps_made "
            "a_x_copied a_prepped a_turned a_turn_sb a_h a_h_sb a_y a_res a_sum a_dev a_sq a_sqsum a_std a_rstd a_out "
            "m_gidx m_turned m_turn_sb m_qkv m_k_sb m_qk m_alpha m_alpha_w m_msg "
            "f_sum f_dev f_sq f_sqsum f_std f_rstd f_out").split()}
        attr_in = slots_of(sem, "attr_in")
        a_in = slots_of(sem, "a_in", slots=4)
        a_stored = slots_of(sem, "a_stored", slots=4)
        m_got = slots_of(sem, "m_got")
        f_in = slots_of(sem, "f_in", slots=4)
        f_stored = slots_of(sem, "f_stored", slots=4)
        chain = [{n: sem(f"{n}_{c}") for n in
                  ("col", "row", "same", "moved", "target", "sum", "pay", "scatter", "landed")}
                 for c in ("s1", "d1", "s2")]

        block = ctx.enter_context(nc.Block())

        def at(i, off):
            return 4 * i + off, off % 2, 2 * i + off // 2

        def exists(step, last):
            return not isinstance(step, int) or 0 <= step <= last

        def reuse(eng, semaphore, count):
            if not isinstance(count, int) or count > 0:
                eng.wait_ge(semaphore, count)

        def v3(tile, n, inner=F):
            return tile.rearrange("p (c f) -> p c f", f=inner)

        @block.sync
        def _(sp):
            for table, a in ((idx_i[0], src), (idx_i[1], dst), (ew, edge_w), (ew2, edge_w2)):
                for n, lo, hi in ((P, 0, T), (P, T, TL), (TAIL, TL, TL + 1)):
                    sp.dma_start(table[0:n, lo:hi], a[P * lo:P * lo + n * (hi - lo)].rearrange(
                        "(p t) -> p t", p=n)).then_inc(S["idx_loaded"], 16)
            sp.wait_ge(S["zero_made"], 1)
            for a in agg:
                sp.dma_start(a.rearrange("n f -> (n f)").rearrange("(p r w) -> p r w", p=P, r=ZR),
                             zeros[:, :].unsqueeze(1).to_broadcast([P, ZR, ZW])).then_inc(S["zeroed"], 16)
            sp.dma_start(acc[N:N + SPARE, :].rearrange("(p g) f -> p (g f)", p=P),
                         zeros[:, 0:G * F]).then_inc(S["zeroed"], 16)
            sp.dma_start(w1[:, :], W1).then_inc(S["dense_consts"], 16)
            sp.dma_start(w2[:, :], W2).then_inc(S["dense_consts"], 16)
            sp.dma_start(b1c[:, :], b1.rearrange("(h o) -> h o", o=1)).then_inc(S["dense_consts"], 16)
            sp.dma_start(b2r[:, :], b2.rearrange("(o f) -> o f", o=1).to_broadcast([P, F])).then_inc(S["dense_consts"], 16)
            sp.wait_ge(S["wqkv_zero"], 1)
            for n, w in enumerate((Wq, Wk, Wv)):
                for h in range(HEADS):
                    sp.dma_start(wqkv[h * FH:(h + 1) * FH, n * F + h * FH:n * F + (h + 1) * FH],
                                 w[h]).then_inc(S["wqkv_loaded"], 16)

            attr_main = edge_attr[0:P * T, :].rearrange("(p t) f -> p (t f)", p=P)

            def load_attr(i, off):
                k, s, _ = at(i, off)
                for c in (0, 1):
                    reuse(sp, chain[c]["sum"], k - 1)
                if is_tail(k):
                    sp.dma_start(attr[s][:, 0:TF * F], edge_attr[P * T:P * TL, :].rearrange(
                        "(p t) f -> p (t f)", p=P)).then_inc(attr_in[s], 16)
                    sp.dma_start(attr[s][0:TAIL, TF * F:(TF + 1) * F], edge_attr[P * TL:E, :]).then_inc(attr_in[s], 16)
                else:
                    sp.dma_start(attr[s][:, :], attr_main[:, bass.ds(k * G * F, G * F)]).then_inc(attr_in[s], 16)

            for n in range(4):
                load_attr(0, n)
            with sp.Fori(1, SB // 4) as i:
                for n in range(4):
                    load_attr(i, n)
            for k in range(SB // 4 * 4, SB + 1):
                load_attr(0, k)

            sp.wait_ge(chain[0]["scatter"], 16 * (TL + 1))
            sp.wait_ge(chain[1]["scatter"], 16 * (TL + 1))

            def load_nodes(i, off):
                q, s, _ = at(i, off)
                reuse(sp, S["a_x_copied"], q - 3)
                reuse(sp, S["a_prepped"], q - 3)
                for tile, a in ((x_in, x), (as_in, agg_src), (ad_in, agg_dst)):
                    sp.dma_start(tile[off % 4][0:rows(q), :], chunk_of(a, q)).then_inc(a_in[off % 4], 16)

            for n in range(8):
                load_nodes(0, n)
            with sp.Fori(2, CHUNKS // 4) as i:
                for n in range(4):
                    load_nodes(i, n)
            for q in range(CHUNKS // 4 * 4, CHUNKS + 1):
                load_nodes(0, q)

            sp.wait_ge(chain[2]["scatter"], 16 * (TL + 1))

            def load_acc(i, off):
                q, s, _ = at(i, off)
                reuse(sp, S["f_dev"], q - 3)
                sp.dma_start(x_in[off % 4][0:rows(q), :], chunk_of(acc, q)).then_inc(f_in[off % 4], 16)

            for n in range(8):
                load_acc(0, n)
            with sp.Fori(2, CHUNKS // 4) as i:
                for n in range(4):
                    load_acc(i, n)
            for q in range(CHUNKS // 4 * 4, CHUNKS + 1):
                load_acc(0, q)
            for s in range(4):
                sp.wait_ge(f_stored[s], 16 * ((CHUNKS - s) // 4 + 1))

        @block.gpsimd
        def _(pool):
            nc.gpsimd.memset(ident[:, :], 0.0).then_inc(S["filled"], 1)
            nc.gpsimd.memset(earlier[:, :], 1.0).then_inc(S["filled"], 1)
            pool.wait_ge(S["filled"], 2)
            nc.gpsimd.affine_select(out=ident[:, :], in_=ident[:, :], compare_op=ALU.not_equal, fill=1.0, base=0,
                                    pattern=[[-1, P]], channel_multiplier=1).then_inc(S["ident_made"], 1)
            own = earlier[:, (G - 1) * P:G * P]
            nc.gpsimd.affine_select(out=own, in_=own, compare_op=ALU.is_ge, fill=0.0, base=0,
                                    pattern=[[-1, P]], channel_multiplier=1).then_inc(S["mask_made"], 1)
            nc.gpsimd.iota(spare_i[:, :], pattern=[[P, G]], base=N, channel_multiplier=1).then_inc(S["spare_made"], 1)

            def scatter(ch, dest, c, i, off):
                k, s, _ = at(i, off)
                sm = chain[ch]
                pool.wait_ge(sm["pay"], k + 1)
                if not isinstance(k, int) or k > 0:
                    pool.wait_ge(sm["scatter"], 16 * G * k)
                    pool.sem_inc(sm["landed"], 1)
                for g in range(tiles(k)):
                    nc.gpsimd.indirect_dma_start(
                        dest[:, :], bass.IndirectOffsetOnAxis(ap=target[c][off % 4][:, g:g + 1], axis=0),
                        pay[c][off % 4][:, g * F:(g + 1) * F], None, compute_op=ALU.add).then_inc(sm["scatter"], 16)

            def sums_step(i, off):
                for c in (0, 1):
                    scatter(c, agg[c], c, i, off)

            pool.wait_ge(S["zeroed"], 48)
            for n in range(4):
                sums_step(0, n)
            with pool.Fori(1, SB // 4) as i:
                for n in range(4):
                    sums_step(i, n)
            for k in range(SB // 4 * 4, SB + 1):
                sums_step(0, k)

            def prep(i, off):
                q, s, m = at(i, off)
                n = rows(q)
                pool.wait_ge(a_in[off % 4], 48 * (i + off // 4 + 1))
                reuse(pool, S["a_turned"], 3 * (q - 1))
                nc.gpsimd.tensor_tensor(xa[s][0:n, :].rearrange("p (c f) -> p c f", c=C)[:, :, F:2 * F],
                                        v3(as_in[off % 4][0:n, :], n), v3(ad_in[off % 4][0:n, :], n), ALU.add)
                reuse(pool, S["a_res"], q - 3)
                nc.gpsimd.tensor_tensor(v3(xb[off % 4][0:n, :], n), v3(x_in[off % 4][0:n, :], n),
                                        b2r[0:n, :].unsqueeze(1).to_broadcast([n, C, F]),
                                        ALU.add).then_inc(S["a_prepped"], 1)

            def scale(pre, stored, per_store, i, off):
                q, s, m = at(i, off)
                n = rows(q)
                pool.wait_ge(S[pre + "rstd"], q + 1)
                reuse(pool, stored[off % 4], per_store * (i + off // 4))
                nc.gpsimd.tensor_tensor(v3(y_out[off % 4][0:n, :], n), v3(dev[s][0:n, :], n),
                                        rstd[s][0:n, :].unsqueeze(2).to_broadcast([n, C, F]),
                                        ALU.mult).then_inc(S[pre + "out"], 1)

            def dense_step(i, off):
                if exists(at(i, off)[0], CHUNKS):
                    prep(i, off)
                if exists(at(i, off - 3)[0], CHUNKS):
                    scale("a_", a_stored, 32, i, off - 3)

            pool.wait_ge(S["dense_consts"], 64)
            for n in range(8):
                dense_step(0, n)
            with pool.Fori(2, CHUNKS // 4) as i:
                for n in range(4):
                    dense_step(i, n)
            for q in range(CHUNKS // 4 * 4, CHUNKS + 4):
                dense_step(0, q)

            def gather(i, off):
                k, s, m = at(i, off)
                for g in range(tiles(k)):
                    n = TAIL if is_tail(k) and g == TF else P
                    nc.gpsimd.indirect_dma_start(
                        xg[off % 4][0:n, g * F:(g + 1) * F], None, x1[:, :],
                        bass.IndirectOffsetOnAxis(ap=gidx[off % 4][0:n, g:g + 1], axis=0)).then_inc(m_got[s], 16)

            def attend_step(i, off):
                k = at(i, off)[0]
                if exists(k, SB):
                    pool.wait_ge(S["m_gidx"], k + 1)
                if exists(at(i, off - 3)[0], SB):
                    scatter(2, acc, 0, i, off - 3)
                if exists(k, SB):
                    gather(i, off)

            for s in range(4):
                pool.wait_ge(a_stored[s], 32 * ((CHUNKS - s) // 4 + 1))
            for n in range(4):
                attend_step(0, n)
            with pool.Fori(1, SB // 4) as i:
                for n in range(4):
                    attend_step(i, n)
            for k in range(SB // 4 * 4, SB + 4):
                attend_step(0, k)

            def last_step(i, off):
                if exists(at(i, off - 2)[0], CHUNKS):
                    scale("f_", f_stored, 16, i, off - 2)

            for n in range(2, 8):
                last_step(0, n)
            with pool.Fori(2, CHUNKS // 4) as i:
                for n in range(4):
                    last_step(i, n)
            for q in range(CHUNKS // 4 * 4, CHUNKS + 3):
                last_step(0, q)

        @block.scalar
        def _(act):
            def stage_col(ch, c, i, off):
                k, s, _ = at(i, off)
                reuse(act, chain[ch]["target"], k - 3)
                nc.scalar.copy(col[c][off % 4][:, 0:tiles(k)], cols(idx_f[c], k)).then_inc(chain[ch]["col"], 1)

            def copy_pay(ch, c, i, off):
                k, s, _ = at(i, off)
                act.wait_ge(chain[ch]["sum"], k + 1)
                act.wait_ge(chain[ch]["target"], k + 1)
                reuse(act, chain[ch]["landed"], k - 3)
                w = tiles(k) * F
                nc.scalar.copy(pay[c][off % 4][:, 0:w], sum_ps[c][s][:, 0:w]).then_inc(chain[ch]["pay"], 1)

            def sums_step(i, off):
                for c in (0, 1):
                    if exists(at(i, off)[0], SB):
                        stage_col(c, c, i, off)
                for c in (0, 1):
                    if exists(at(i, off - 1)[0], SB):
                        copy_pay(c, c, i, off - 1)

            act.wait_ge(S["tables_made"], 1)
            for n in range(4):
                sums_step(0, n)
            with act.Fori(1, SB // 4) as i:
                for n in range(4):
                    sums_step(i, n)
            for k in range(SB // 4 * 4, SB + 2):
                sums_step(0, k)

            def copy_turned(i, n3):
                q, g, u = 4 * i + n3 // 3, n3 % 3, n3 % 2
                w = GROUPS[g][1] * rows(q)
                act.wait_ge(S["a_turned"], 3 * q + g + 1)
                reuse(act, S["a_h"], 3 * q + g - 1)
                nc.scalar.copy(xaT[u][:, 0:w], xaT_ps[u][:, 0:w]).then_inc(S["a_turn_sb"], 1)

            def relu(i, n3):
                q, g, u = 4 * i + n3 // 3, n3 % 3, n3 % 2
                if not exists(q, CHUNKS):
                    return
                w = GROUPS[g][1] * rows(q)
                act.wait_ge(S["a_h"], 3 * q + g + 1)
                reuse(act, S["a_y"], 3 * q + g - 1)
                nc.scalar.activation(hT[u][:, 0:w], h_ps[u][:, 0:w], ACT.Relu,
                                     bias=b1c[:, 0:1]).then_inc(S["a_h_sb"], 1)

            def square(pre, i, off):
                q, s, _ = at(i, off)
                if not exists(q, CHUNKS):
                    return
                n = rows(q)
                act.wait_ge(S[pre + "dev"], q + 1)
                reuse(act, S[pre + "sqsum"], q - 1)
                nc.scalar.activation(sq[s][0:n, :], dev[s][0:n, :], ACT.Square).then_inc(S[pre + "sq"], 1)

            def root(pre, i, off):
                q, s, _ = at(i, off)
                if not exists(q, CHUNKS):
                    return
                n = rows(q)
                act.wait_ge(S[pre + "sqsum"], q + 1)
                reuse(act, S[pre + "rstd"], q - 1)
                nc.scalar.activation(std[s][0:n, :], sqsum[s][0:n, :], ACT.Sqrt, scale=1.0 / F,
                                     bias=eps[0:n, 0:1]).then_inc(S[pre + "std"], 1)

            def store(pre, dests, stored, i, off):
                q, s, _ = at(i, off)
                if not exists(q, CHUNKS):
                    return
                act.wait_ge(S[pre + "out"], q + 1)
                for dest in dests:
                    act.dma_start(chunk_of(dest, q), y_out[off % 4][0:rows(q), :]).then_inc(stored[off % 4], 16)

            def dense_step(i, off):
                here = exists(at(i, off)[0], CHUNKS)
                for g in range(3):
                    if here:
                        copy_turned(i, 3 * off + g)
                    relu(i, 3 * off + g - 1)
                    if g == 0:
                        square("a_", i, off - 2)
                root("a_", i, off - 2)
                store("a_", (x1, acc), a_stored, i, off - 3)

            act.wait_ge(S["dense_consts"], 64)
            act.wait_ge(S["eps_made"], 1)
            for n in range(8):
                dense_step(0, n)
            with act.Fori(2, CHUNKS // 4) as i:
                for n in range(4):
                    dense_step(i, n)
            for q in range(CHUNKS // 4 * 4, CHUNKS + 4):
                dense_step(0, q)

            def stage_gather(i, off):
                k, s, m = at(i, off)
                reuse(act, m_got[s], 16 * G * m)
                reuse(act, S["m_turned"], k - 3)
                nc.scalar.copy(gidx[off % 4][:, 0:tiles(k)], cols(idx_f[1], k)).then_inc(S["m_gidx"], 1)

            def copy_edges(i, off):
                k, s, _ = at(i, off)
                w = tiles(k)
                act.wait_ge(S["m_turned"], k + 1)
                reuse(act, S["m_qkv"], k - 1)
                nc.scalar.copy(xgT[s][:, 0:w * P], xgT_ps[s][:, 0:w * P]).then_inc(S["m_turn_sb"], 1)
                act.wait_ge(S["m_qkv"], k + 1)
                reuse(act, S["m_qk"], k - 1)
                nc.scalar.copy(v3(k_sb[s][:, 0:w * F], P), qkv_ps[s][:, 0:w, F:2 * F]).then_inc(S["m_k_sb"], 1)

            def attend_step(i, off):
                if exists(at(i, off)[0], SB):
                    stage_col(2, 0, i, off)
                if exists(at(i, off + 2)[0], SB):
                    stage_gather(i, off + 2)
                if exists(at(i, off)[0], SB):
                    copy_edges(i, off)
                if exists(at(i, off - 1)[0], SB):
                    copy_pay(2, 0, i, off - 1)

            stage_gather(0, 0)
            stage_gather(0, 1)
            for n in range(4):
                attend_step(0, n)
            with act.Fori(1, SB // 4 - 1) as i:
                for n in range(4):
                    attend_step(i, n)
            for k in range(SB // 4 * 4 - 4, SB + 2):
                attend_step(0, k)

            def last_step(i, off):
                root("f_", i, off - 1)
                square("f_", i, off)
                store("f_", (out,), f_stored, i, off - 2)

            for n in range(8):
                last_step(0, n)
            with act.Fori(2, CHUNKS // 4) as i:
                for n in range(4):
                    last_step(i, n)
            for q in range(CHUNKS // 4 * 4, CHUNKS + 3):
                last_step(0, q)

        @block.tensor
        def _(pe):
            def turn_cols(ch, c, i, off):
                k, s, _ = at(i, off)
                pe.wait_ge(chain[ch]["col"], k + 1)
                reuse(pe, chain[ch]["same"], k - 1)
                for g in range(tiles(k)):
                    last = nc.tensor.transpose(row_ps[c][s][:, g * P:(g + 1) * P],
                                               col[c][off % 4][:, g:g + 1].to_broadcast([P, P]), ident[:, :])
                last.then_inc(chain[ch]["row"], 1)

            def sum_same(ch, c, rows_of, i, off):
                k, s, _ = at(i, off)
                pe.wait_ge(chain[ch]["same"], k + 1)
                reuse(pe, chain[ch]["pay"], k - 1)
                for a in range(tiles(k)):
                    for b in range(a, tiles(k)):
                        at_b = b * G * P + a * P
                        last = nc.tensor.matmul(sum_ps[c][s][:, a * F:(a + 1) * F], same[c][s][:, at_b:at_b + P],
                                                rows_of[s][:, b * F:(b + 1) * F],
                                                start=(b == a), stop=(b == tiles(k) - 1))
                last.then_inc(chain[ch]["sum"], 1)

            def sums_step(i, off):
                for c in (0, 1):
                    if exists(at(i, off)[0], SB):
                        turn_cols(c, c, i, off)
                if exists(at(i, off - 1)[0], SB):
                    _, s, m = at(i, off - 1)
                    pe.wait_ge(attr_in[s], 16 * (m + 1) + 16 * is_tail(at(i, off - 1)[0]))
                    for c in (0, 1):
                        sum_same(c, c, attr, i, off - 1)

            pe.wait_ge(S["ident_made"], 1)
            for n in range(4):
                sums_step(0, n)
            with pe.Fori(1, SB // 4) as i:
                for n in range(4):
                    sums_step(i, n)
            for k in range(SB // 4 * 4, SB + 2):
                sums_step(0, k)

            def turn_nodes(i, n3):
                q, g, u = 4 * i + n3 // 3, n3 % 3, n3 % 2
                if not exists(q, CHUNKS):
                    return
                s, n = (n3 // 3) % 2, rows(q)
                if g == 0:
                    pe.wait_ge(S["a_x_copied"], q + 1)
                    pe.wait_ge(S["a_prepped"], q + 1)
                reuse(pe, S["a_turn_sb"], 3 * q + g - 1)
                c0, nc_ = GROUPS[g]
                for c in range(nc_):
                    last = nc.tensor.transpose(xaT_ps[u][:, c * n:(c + 1) * n],
                                               xa[s][0:n, (c0 + c) * 2 * F:(c0 + c + 1) * 2 * F], ident[0:n, 0:n])
                last.then_inc(S["a_turned"], 1)

            def hidden(i, n3):
                q, g, u = 4 * i + n3 // 3, n3 % 3, n3 % 2
                if not exists(q, CHUNKS):
                    return
                w = GROUPS[g][1] * rows(q)
                pe.wait_ge(S["a_turn_sb"], 3 * q + g + 1)
                reuse(pe, S["a_h_sb"], 3 * q + g - 1)
                nc.tensor.matmul(h_ps[u][:, 0:w], w1[:, :], xaT[u][:, 0:w], start=True,
                                 stop=True).then_inc(S["a_h"], 1)

            def project(i, n3):
                q, g, u = 4 * i + n3 // 3, n3 % 3, n3 % 2
                if not exists(q, CHUNKS):
                    return
                s, n = (n3 // 3) % 2, rows(q)
                pe.wait_ge(S["a_h_sb"], 3 * q + g + 1)
                if g == 0:
                    reuse(pe, S["a_res"], q - 1)
                c0, nc_ = GROUPS[g]
                for c in range(nc_):
                    half, at_c = (c0 + c) // HALF, (c0 + c) % HALF * F
                    last = nc.tensor.matmul(y_ps[s][half][0:n, at_c:at_c + F], hT[u][:, c * n:(c + 1) * n],
                                            w2[:, :], start=True, stop=True)
                last.then_inc(S["a_y"], 1)

            def dense_step(i, off):
                for g in range(3):
                    turn_nodes(i, 3 * off + g)
                    hidden(i, 3 * off + g - 1)
                    project(i, 3 * off + g - 2)

            pe.wait_ge(S["dense_consts"], 64)
            for n in range(8):
                dense_step(0, n)
            with pe.Fori(2, CHUNKS // 4) as i:
                for n in range(4):
                    dense_step(i, n)
            for q in range(CHUNKS // 4 * 4, CHUNKS + 2):
                dense_step(0, q)

            def turn_edges(i, off):
                k, s, m = at(i, off)
                for g in range(tiles(k)):
                    last = nc.tensor.transpose(xgT_ps[s][:, g * P:(g + 1) * P], xg[off % 4][:, g * F:(g + 1) * F],
                                               ident[:, :])
                last.then_inc(S["m_turned"], 1)

            def project_edges(i, off):
                k, s, m = at(i, off)
                pe.wait_ge(S["m_turn_sb"], k + 1)
                for g in range(tiles(k)):
                    last = nc.tensor.matmul(qkv_ps[s][:, g, 0:3 * F], xgT[s][:, g * P:(g + 1) * P], wqkv[:, :],
                                            start=True, stop=True)
                last.then_inc(S["m_qkv"], 1)

            def attend_step(i, off):
                k, s, m = at(i, off)
                if exists(k, SB):
                    pe.wait_ge(m_got[s], 16 * G * m + 16 * tiles(k))
                    reuse(pe, S["m_msg"], k - 1)
                    turn_cols(2, 0, i, off)
                    turn_edges(i, off)
                if exists(at(i, off - 1)[0], SB):
                    pe.wait_ge(S["m_msg"], at(i, off - 1)[0] + 1)
                    sum_same(2, 0, msg, i, off - 1)
                if exists(k, SB):
                    project_edges(i, off)

            pe.wait_ge(S["wqkv_loaded"], 16 * 3 * HEADS)
            for n in range(4):
                attend_step(0, n)
            with pe.Fori(1, SB // 4) as i:
                for n in range(4):
                    attend_step(i, n)
            for k in range(SB // 4 * 4, SB + 2):
                attend_step(0, k)

        @block.vector
        def _(dve):
            nc.vector.memset(zeros[:, :], 0.0).then_inc(S["zero_made"], 1)
            nc.vector.memset(wqkv[:, :], 0.0).then_inc(S["wqkv_zero"], 1)
            nc.vector.memset(eps[:, :], EPS).then_inc(S["eps_made"], 1)
            nc.vector.memset(weight[:, TL:TL + 1], 0.0)
            dve.wait_ge(S["spare_made"], 1)
            nc.vector.tensor_copy(spare_f[:, :], spare_i[:, :]).then_inc(S["table_step"], 1)
            dve.wait_ge(S["table_step"], 1)
            dve.wait_ge(S["idx_loaded"], 16 * 12)
            for c in (0, 1):
                nc.vector.tensor_copy(idx_f[c][:, 0:TL], idx_i[c][:, 0:TL])
                nc.vector.tensor_copy(idx_f[c][:, TL:TL + 1], spare_f[:, TF:TF + 1]).then_inc(S["table_step"], 1)
            dve.wait_ge(S["table_step"], 3)
            for c in (0, 1):
                nc.vector.tensor_copy(idx_f[c][0:TAIL, TL:TL + 1],
                                      idx_i[c][0:TAIL, TL:TL + 1]).then_inc(S["table_step"], 1)
            for n, lo, hi in ((P, 0, TL), (TAIL, TL, TL + 1)):
                nc.vector.scalar_tensor_tensor(out=weight[0:n, lo:hi], in0=ew[0:n, lo:hi], scalar=float(FH) ** -0.5,
                                               in1=ew2[0:n, lo:hi], op0=ALU.mult, op1=ALU.mult)
            dve.wait_ge(S["table_step"], 5)
            for c in (0, 1):
                nc.vector.tensor_tensor(to_spare[c][:, 0:T].rearrange("p (k g) -> p k g", g=G),
                                        spare_f[:, :].unsqueeze(1).to_broadcast([P, SB, G]),
                                        idx_f[c][:, 0:T].rearrange("p (k g) -> p k g", g=G), ALU.subtract)
                last = nc.vector.tensor_tensor(to_spare[c][:, T:TL + 1], spare_f[:, 0:TF + 1],
                                               idx_f[c][:, T:TL + 1], ALU.subtract)
            last.then_inc(S["tables_made"], 1)
            dve.wait_ge(S["tables_made"], 1)
            dve.wait_ge(S["mask_made"], 1)

            def compare(ch, c, i, off):
                k, s, _ = at(i, off)
                sm, t = chain[ch], tiles(k)
                dve.wait_ge(sm["row"], k + 1)
                reuse(dve, sm["sum"], k - 1)
                for b in range(t):
                    w = (b + 1) * P
                    last = nc.vector.scalar_tensor_tensor(
                        out=same[c][s][:, b * G * P:b * G * P + w], in0=row_ps[c][s][:, 0:w],
                        scalar=col[c][off % 4][:, b:b + 1], in1=earlier[:, G * P - w:G * P],
                        op0=ALU.is_equal, op1=ALU.mult, accum_out=rank[c][s][:, b:b + 1])
                last.then_inc(sm["same"], 1)
                dve.wait_ge(sm["same"], k + 1)
                nc.vector.scalar_tensor_tensor(out=move[c][off % 4][:, 0:t], in0=rank[c][s][:, 0:t], scalar=1.5,
                                               in1=cols(to_spare[c], k), op0=ALU.is_gt,
                                               op1=ALU.mult).then_inc(sm["moved"], 1)
                dve.wait_ge(sm["moved"], k + 1)
                reuse(dve, sm["landed"], k - 3)
                nc.vector.tensor_tensor(target[c][off % 4][:, 0:t], move[c][off % 4][:, 0:t], col[c][off % 4][:, 0:t],
                                        ALU.add).then_inc(sm["target"], 1)

            def sums_step(i, off):
                for c in (0, 1):
                    compare(c, c, i, off)

            for n in range(4):
                sums_step(0, n)
            with dve.Fori(1, SB // 4) as i:
                for n in range(4):
                    sums_step(i, n)
            for k in range(SB // 4 * 4, SB + 1):
                sums_step(0, k)

            def deviate(pre, value, i, off):
                q, s, _ = at(i, off)
                n = rows(q)
                nc.vector.tensor_reduce(total[s][0:n, :], v3(value[0:n, :], n), AX_X,
                                        ALU.add).then_inc(S[pre + "sum"], 1)
                dve.wait_ge(S[pre + "sum"], q + 1)
                reuse(dve, S[pre + "out"], q - 1)
                nc.vector.scalar_tensor_tensor(out=v3(dev[s][0:n, :], n),
                                               in0=total[s][0:n, :].unsqueeze(2).to_broadcast([n, C, F]),
                                               scalar=-1.0 / F, in1=v3(value[0:n, :], n), op0=ALU.mult,
                                               op1=ALU.add).then_inc(S[pre + "dev"], 1)

            def sum_squares(pre, i, off):
                q, s, _ = at(i, off)
                if not exists(q, CHUNKS):
                    return
                n = rows(q)
                dve.wait_ge(S[pre + "sq"], q + 1)
                nc.vector.tensor_reduce(sqsum[s][0:n, :], v3(sq[s][0:n, :], n), AX_X,
                                        ALU.add).then_inc(S[pre + "sqsum"], 1)

            def invert(pre, i, off):
                q, s, _ = at(i, off)
                if not exists(q, CHUNKS):
                    return
                n = rows(q)
                dve.wait_ge(S[pre + "std"], q + 1)
                nc.vector.reciprocal(rstd[s][0:n, :], std[s][0:n, :]).then_inc(S[pre + "rstd"], 1)

            def copy_x(i, off):
                q, s, m = at(i, off)
                n = rows(q)
                dve.wait_ge(a_in[off % 4], 48 * (i + off // 4 + 1))
                reuse(dve, S["a_turned"], 3 * (q - 1))
                nc.vector.tensor_copy(xa[s][0:n, :].rearrange("p (c f) -> p c f", c=C)[:, :, 0:F],
                               v3(x_in[off % 4][0:n, :], n)).then_inc(S["a_x_copied"], 1)

            def dense_step(i, off):
                if exists(at(i, off + 2)[0], CHUNKS):
                    copy_x(i, off + 2)
                sum_squares("a_", i, off - 1)
                q, s, _ = at(i, off)
                if exists(q, CHUNKS):
                    n = rows(q)
                    dve.wait_ge(S["a_prepped"], q + 1)
                    dve.wait_ge(S["a_y"], 3 * q + 3)
                    for half in (0, 1):
                        lo = half * HALF * F
                        last = nc.vector.tensor_tensor(res[s][0:n, lo:lo + HALF * F], y_ps[s][half][0:n, 0:HALF * F],
                                                       xb[off % 4][0:n, lo:lo + HALF * F], ALU.add)
                    last.then_inc(S["a_res"], 1)
                    dve.wait_ge(S["a_res"], q + 1)
                    deviate("a_", res[s], i, off)
                invert("a_", i, off - 1)

            copy_x(0, 0)
            copy_x(0, 1)

            for n in range(8):
                dense_step(0, n)
            with dve.Fori(2, CHUNKS // 4) as i:
                for n in range(4):
                    dense_step(i, n)
            for q in range(CHUNKS // 4 * 4, CHUNKS + 2):
                dense_step(0, q)

            def message(i, off):
                k, s, _ = at(i, off)
                t = tiles(k)
                dve.wait_ge(S["m_k_sb"], k + 1)
                nc.vector.tensor_tensor(v3(qk[s][:, 0:t * F], P),
                                        qkv_ps[s][:, 0:t, 0:F],
                                        v3(k_sb[s][:, 0:t * F], P), ALU.mult).then_inc(S["m_qk"], 1)
                dve.wait_ge(S["m_qk"], k + 1)
                nc.vector.tensor_reduce(alpha[s][:, 0:t * HEADS],
                                        qk[s][:, 0:t * F].rearrange("p (h f) -> p h f", f=FH), AX_X,
                                        ALU.add).then_inc(S["m_alpha"], 1)
                dve.wait_ge(S["m_alpha"], k + 1)
                nc.vector.tensor_tensor(alpha_w[s][:, 0:t * HEADS].rearrange("p (g h) -> p g h", h=HEADS),
                                        alpha[s][:, 0:t * HEADS].rearrange("p (g h) -> p g h", h=HEADS),
                                        cols(weight, k).unsqueeze(2).to_broadcast([P, t, HEADS]),
                                        ALU.mult).then_inc(S["m_alpha_w"], 1)
                dve.wait_ge(S["m_alpha_w"], k + 1)
                nc.vector.tensor_tensor(msg[s][:, 0:t * F].rearrange("p (g h f) -> p g h f", g=t, f=FH),
                                        qkv_ps[s][:, 0:t, 2 * F:3 * F].rearrange("p g (h f) -> p g h f", f=FH),
                                        alpha_w[s][:, 0:t * HEADS].rearrange("p (g h) -> p g h", h=HEADS)
                                        .unsqueeze(3).to_broadcast([P, t, HEADS, FH]),
                                        ALU.mult).then_inc(S["m_msg"], 1)

            def attend_step(i, off):
                compare(2, 0, i, off)
                message(i, off)

            for n in range(4):
                attend_step(0, n)
            with dve.Fori(1, SB // 4) as i:
                for n in range(4):
                    attend_step(i, n)
            for k in range(SB // 4 * 4, SB + 1):
                attend_step(0, k)

            def last_step(i, off):
                q, s, m = at(i, off)
                sum_squares("f_", i, off - 1)
                if exists(q, CHUNKS):
                    dve.wait_ge(f_in[off % 4], 16 * (i + off // 4 + 1))
                    deviate("f_", x_in[off % 4], i, off)
                invert("f_", i, off - 1)

            for n in range(8):
                last_step(0, n)
            with dve.Fori(2, CHUNKS // 4) as i:
                for n in range(4):
                    last_step(i, n)
            for q in range(CHUNKS // 4 * 4, CHUNKS + 3):
                last_step(0, q)


_INS = ["x", "src", "dst", "edge_attr_64", "edge_weight", "edge_weight_n2", "L0_gnn_W1", "L0_gnn_b1", "L0_gnn_W2",
        "L0_gnn_b2", "L1_gnn_Wq", "L1_gnn_Wk", "L1_gnn_Wv"]


def kernel(**inputs):
    import numpy as _np
    import concourse.bacc as _bacc
    from concourse import mybir as _mybir
    from concourse.bass_utils import run_bass_kernel_spmd as _run

    nc = _bacc.Bacc("TRN2", target_bir_lowering=False, num_devices=1)
    arrays, args = {}, []
    for name in _INS:
        a = _np.ascontiguousarray(inputs[name])
        arrays[f"in_{name}"] = a
        args.append(nc.dram_tensor(f"in_{name}", a.shape, _mybir.dt.from_np(a.dtype), kind="ExternalInput").ap())
    out = nc.dram_tensor("out_0", inputs["x"].shape, _mybir.dt.float32, kind="ExternalOutput").ap()
    build(nc, *args, out)
    r = _run(nc, [arrays], core_ids=[0])
    return r.results[0]["out_0"]
```

```python
from contextlib import ExitStack

import concourse.bass as bass
from concourse import mybir

F32 = mybir.dt.float32
BF16 = mybir.dt.bfloat16
I32 = mybir.dt.int32
ALU = mybir.AluOpType
ACT = mybir.ActivationFunctionType
AX_X = mybir.AxisListType.X

P = 128
G = 4
C = 10
LC = 2 * C
SHARED = 12
GROUPS = [(0, 4), (4, 4), (8, 2)]
EPS = 1e-5


def build(nc, x, src, dst, edge_attr, edge_w, edge_w2, W1, b1, W2, b2, Wq, Wk, Wv, out):
    N, F = x.shape
    E = edge_attr.shape[0]
    HID = W1.shape[1]
    HEADS, FH, _ = Wq.shape

    SB = E // P // G
    T = SB * G
    TF = E // P - T
    TL = T + TF
    TAIL = E - P * TL
    assert 0 < TF < G and 0 < TAIL < P
    CHUNKS = N // P // (2 * C) * 2
    COLS = CHUNKS * C
    REST = (N - P * COLS) // C
    assert REST * C == N - P * COLS and 0 < REST <= 32 and CHUNKS % 4 == 2
    SPARE = G * P
    CF = C * F
    LCHUNKS = CHUNKS // 2

    agg_src = nc.dram_tensor("agg_src", (N + SPARE, F), F32).ap()
    agg_dst = nc.dram_tensor("agg_dst", (N + SPARE, F), F32).ap()
    agg = [agg_src, agg_dst]
    x1 = nc.dram_tensor("x1", (N, F), F32).ap()
    acc = nc.dram_tensor("acc", (N + SPARE, F), F32).ap()

    def main_nodes(a):
        return a[0:P * COLS, :].rearrange("(p j) f -> p (j f)", p=P)

    def rest_nodes(a):
        return a[P * COLS:N, :].rearrange("(p j) f -> p (j f)", p=REST)

    passes = {"a_": (CHUNKS, C), "f_": (LCHUNKS, LC)}

    def size(pre, q):
        last, nodes = passes[pre]
        return (REST, C) if isinstance(q, int) and q == last else (P, nodes)

    def rows(q):
        return size("a_", q)[0]

    def chunk_of(pre, a, q):
        last, nodes = passes[pre]
        if isinstance(q, int) and q == last:
            return rest_nodes(a)
        return main_nodes(a)[:, bass.ds(q * nodes * F, nodes * F)]

    def is_tail(k):
        return isinstance(k, int) and k == SB

    def tiles(k):
        return TF + 1 if is_tail(k) else G

    def cols(table, k):
        return table[:, T:TL + 1] if is_tail(k) else table[:, bass.ds(k * G, G)]

    ZR = 2 * SHARED
    ZW = (N + SPARE) * F // P // ZR
    assert ZW * P * ZR == (N + SPARE) * F and ZW >= G * F and SHARED % 4 == 0

    with ExitStack() as ctx:
        def sb(name, shape, dt=F32):
            return ctx.enter_context(nc.sbuf_tensor(name, shape, dt))

        def sem(name):
            return ctx.enter_context(nc.semaphore(name))

        def slots_of(make, name, *args, slots=2):
            return [make(f"{name}{n}", *args) for n in range(slots)]

        def for_chains(make, name, *args, slots=2):
            return [slots_of(make, f"{name}{c}_", *args, slots=slots) for c in "sd"]

        zeros = sb("zeros", [P, ZW])
        ident = sb("ident", [P, P])
        earlier = sb("earlier", [P, G * P])
        w1 = sb("w1", [2 * F, HID])
        w2 = sb("w2", [HID, F])
        b1c = sb("b1c", [HID, 1])
        b2r = sb("b2r", [P, F])
        wqkv = sb("wqkv", [F, 3 * F])
        eps = sb("eps", [P, 1])
        idx_i = [sb("src_i", [P, TL + 1], I32), sb("dst_i", [P, TL + 1], I32)]
        idx_f = [sb("src_f", [P, TL + 1]), sb("dst_f", [P, TL + 1])]
        to_spare = [sb("src_spare", [P, TL + 1]), sb("dst_spare", [P, TL + 1])]
        spare_i = sb("spare_i", [P, G], I32)
        spare_f = sb("spare_f", [P, G])
        ew = sb("ew", [P, TL + 1])
        ew2 = sb("ew2", [P, TL + 1])
        weight = sb("weight", [P, TL + 1])

        attr = slots_of(sb, "attr", [P, G * F])
        col = for_chains(sb, "col", [P, G], slots=4)
        same = for_chains(sb, "same", [P, G * G * P], BF16)
        parts = slots_of(sb, "parts", [P, 3, G * F], BF16)
        left = slots_of(sb, "left", [P, G * F])
        rank = for_chains(sb, "rank", [P, G])
        move = for_chains(sb, "move", [P, G], slots=4)
        target = for_chains(sb, "target", [P, G], I32, slots=4)
        pay = for_chains(sb, "pay", [P, G * F], slots=4)
        gidx = slots_of(sb, "gidx", [P, G], I32, slots=4)
        xg = slots_of(sb, "xg", [P, G * F], slots=4)
        xgT = slots_of(sb, "xgT", [F, G * P])
        k_sb = slots_of(sb, "k_sb", [P, G * F])
        qk = slots_of(sb, "qk", [P, G * F])
        alpha = slots_of(sb, "alpha", [P, G * HEADS])
        alpha_w = slots_of(sb, "alpha_w", [P, G * HEADS])
        msg = slots_of(sb, "msg", [P, G * F])

        def views(tile, n):
            w = tile.shape[1] // n
            return [tile[:, k * w:(k + 1) * w] for k in range(n)]

        sums_in = sb("sums_in", [P, 8 * CF])
        to_turn_or_dev = sb("to_turn_or_dev", [P, 8 * CF])
        x_or_out = sb("x_or_out", [P, 8 * CF])
        as_in, ad_in = views(sums_in, 8)[0:4], views(sums_in, 8)[4:8]
        xa = views(to_turn_or_dev, 4)
        x_in, xb = views(x_or_out, 8)[0:4], views(x_or_out, 8)[4:8]
        xaT = slots_of(sb, "xaT", [2 * F, 4 * P])
        hT = slots_of(sb, "hT", [HID, 4 * P])
        res = slots_of(sb, "res", [P, CF])
        dev = slots_of(sb, "dev", [P, CF], slots=4)
        sq = slots_of(sb, "sq", [P, LC * F])
        total = slots_of(sb, "total", [P, LC])
        sqsum = slots_of(sb, "sqsum", [P, LC])
        std = slots_of(sb, "std", [P, LC])
        folded = slots_of(sb, "folded", [P, LC * F // 2])
        rstd = slots_of(sb, "rstd", [P, LC], slots=4)
        y_out = slots_of(sb, "y_out", [P, CF], slots=4)

        last_in = views(sums_in, 4)
        norm = {"a_": (dev, y_out), "f_": (views(to_turn_or_dev, 4), views(x_or_out, 4))}

        pairs = [ctx.enter_context(nc.psum_tensor(f"pair{b}", [P, 1024], F32)) for b in range(4)]
        banks = [pairs[b // 2][:, b % 2 * 512:b % 2 * 512 + 512] for b in range(8)]
        row_ps = [[banks[0], banks[1]], [banks[2], banks[3]]]
        sum_ps = [[banks[4], banks[5]], [banks[6], banks[7]]]
        QKV = 256
        qkv_ps = [pairs[1][:, 0:G * QKV].rearrange("p (g f) -> p g f", f=QKV),
                  pairs[3][:, 0:G * QKV].rearrange("p (g f) -> p g f", f=QKV)]
        xgT_ps = [pairs[1][0:F, 0:G * P], pairs[3][0:F, 0:G * P]]
        xaT_ps = banks[0:2]
        h_ps = banks[2:4]
        y_ps = [banks[4:6], banks[6:8]]
        HALF = C // 2

        S = {name: sem(name) for name in (
            "zero_made src_zeroed dst_zeroed dense_consts idx_loaded filled ident_made mask_made spare_made table_step tables_made "
            "wqkv_zero wqkv_loaded eps_made "
            "a_x_copied a_prepped a_turned a_turn_sb a_h a_h_sb a_y a_res a_sum a_dev a_sq a_sqsum a_std a_rstd a_out "
            "attr_high attr_left attr_mid attr_split msg_high msg_left msg_mid msg_split "
            "m_gidx m_turned m_turn_sb m_qkv m_k_sb m_qk m_alpha m_alpha_w m_msg "
            "f_fold f_sum f_dev f_sq f_sqsum f_std f_rstd f_out").split()}
        attr_in = slots_of(sem, "attr_in")
        a_in = slots_of(sem, "a_in", slots=4)
        a_stored = slots_of(sem, "a_stored", slots=4)
        m_got = slots_of(sem, "m_got")
        f_in = slots_of(sem, "f_in", slots=4)
        f_stored = slots_of(sem, "f_stored", slots=4)
        chain = [{n: sem(f"{n}_{c}") for n in
                  ("col", "row", "same", "moved", "target", "sum", "pay", "scatter", "landed")}
                 for c in ("s1", "d1", "s2")]

        block = ctx.enter_context(nc.Block())

        def at(i, off):
            return 4 * i + off, off % 2, 2 * i + off // 2

        def exists(step, last):
            return not isinstance(step, int) or 0 <= step <= last

        def reuse(eng, semaphore, count):
            if not isinstance(count, int) or count > 0:
                eng.wait_ge(semaphore, count)

        def v3(tile, n, inner=F):
            return tile.rearrange("p (c f) -> p c f", f=inner)

        @block.sync
        def _(sp):
            def clear(a, first, runs, zeroed):
                share = a.rearrange("n f -> (n f)").rearrange("(p r w) -> p r w", p=P, r=ZR)
                sp.dma_start(share[:, bass.ds(first, runs), :],
                             zeros[:, :].unsqueeze(1).to_broadcast([P, runs, ZW])).then_inc(zeroed, 16)

            sp.wait_ge(S["zero_made"], 1)
            clear(agg_src, 0, ZR // 2, S["src_zeroed"])
            for table, a in ((idx_i[0], src), (idx_i[1], dst), (ew, edge_w), (ew2, edge_w2)):
                for n, lo, hi in ((P, 0, T), (P, T, TL), (TAIL, TL, TL + 1)):
                    sp.dma_start(table[0:n, lo:hi], a[P * lo:P * lo + n * (hi - lo)].rearrange(
                        "(p t) -> p t", p=n)).then_inc(S["idx_loaded"], 16)
            attr_main = edge_attr[0:P * T, :].rearrange("(p t) f -> p (t f)", p=P)

            def load_attr(i, off):
                k, s, _ = at(i, off)
                reuse(sp, S["attr_split"], k - 1)
                if is_tail(k):
                    sp.dma_start(attr[s][:, 0:TF * F], edge_attr[P * T:P * TL, :].rearrange(
                        "(p t) f -> p (t f)", p=P)).then_inc(attr_in[s], 16)
                    sp.dma_start(attr[s][0:TAIL, TF * F:(TF + 1) * F], edge_attr[P * TL:E, :]).then_inc(attr_in[s], 16)
                else:
                    sp.dma_start(attr[s][:, :], attr_main[:, bass.ds(k * G * F, G * F)]).then_inc(attr_in[s], 16)

            load_attr(0, 0)
            load_attr(0, 1)

            clear(agg_src, ZR // 2, ZR - ZR // 2, S["src_zeroed"])
            sp.dma_start(acc[N:N + SPARE, :].rearrange("(p g) f -> p (g f)", p=P),
                         zeros[:, 0:G * F]).then_inc(S["dst_zeroed"], 16)
            sp.wait_ge(S["src_zeroed"], 32)
            def shared_step(i, off):
                k, s, _ = at(i, off)
                load_attr(i, off + 2)
                reuse(sp, chain[1]["scatter"], 16 * G * k)
                clear(agg_dst, 2 * k, 1, S["dst_zeroed"])
                sp.wait_ge(chain[0]["scatter"], 16 * G * k + 16 * G)
                clear(agg_dst, 2 * k + 1, 1, S["dst_zeroed"])

            for n in range(4):
                shared_step(0, n)
            with sp.Fori(1, SHARED // 4) as i:
                for n in range(4):
                    shared_step(i, n)
            with sp.Fori(SHARED // 4, SB // 4 - 1) as i:
                for n in range(4):
                    load_attr(i, n + 2)
            for k in range(SB // 4 * 4 - 2, SB + 1):
                load_attr(0, k)

            sp.wait_ge(chain[0]["scatter"], 16 * (TL + 1))
            sp.wait_ge(chain[1]["scatter"], 16 * (TL + 1))

            def load_nodes(i, off):
                q, s, _ = at(i, off)
                reuse(sp, S["a_x_copied"], q - 3)
                reuse(sp, S["a_prepped"], q - 3)
                for tile, a in ((x_in, x), (as_in, agg_src), (ad_in, agg_dst)):
                    sp.dma_start(tile[off % 4][0:rows(q), :], chunk_of("a_", a, q)).then_inc(a_in[off % 4], 16)

            for n in range(8):
                load_nodes(0, n)
            with sp.Fori(2, CHUNKS // 4) as i:
                for n in range(4):
                    load_nodes(i, n)
            for q in range(CHUNKS // 4 * 4, CHUNKS + 1):
                load_nodes(0, q)

            sp.wait_ge(chain[2]["scatter"], 16 * (TL + 1))

            def load_acc(i, off):
                q, s, _ = at(i, off)
                reuse(sp, S["f_dev"], q - 3)
                reuse(sp, S["f_fold"], q - 3)
                n, c = size("f_", q)
                sp.dma_start(last_in[off % 4][0:n, 0:c * F], chunk_of("f_", acc, q)).then_inc(f_in[off % 4], 16)

            for n in range(8):
                load_acc(0, n)
            with sp.Fori(2, LCHUNKS // 4) as i:
                for n in range(4):
                    load_acc(i, n)
            for q in range(LCHUNKS // 4 * 4, LCHUNKS + 1):
                load_acc(0, q)
            for s in range(4):
                sp.wait_ge(f_stored[s], 16 * ((LCHUNKS - s) // 4 + 1))

        @block.gpsimd
        def _(pool):
            nc.gpsimd.memset(ident[:, :], 0.0).then_inc(S["filled"], 1)
            nc.gpsimd.memset(earlier[:, :], 1.0).then_inc(S["filled"], 1)
            pool.wait_ge(S["filled"], 2)
            nc.gpsimd.affine_select(out=ident[:, :], in_=ident[:, :], compare_op=ALU.not_equal, fill=1.0, base=0,
                                    pattern=[[-1, P]], channel_multiplier=1).then_inc(S["ident_made"], 1)
            own = earlier[:, (G - 1) * P:G * P]
            nc.gpsimd.affine_select(out=own, in_=own, compare_op=ALU.is_ge, fill=0.0, base=0,
                                    pattern=[[-1, P]], channel_multiplier=1).then_inc(S["mask_made"], 1)
            nc.gpsimd.iota(spare_i[:, :], pattern=[[P, G]], base=N, channel_multiplier=1).then_inc(S["spare_made"], 1)

            def scatter(ch, dest, c, i, off):
                k, s, _ = at(i, off)
                sm = chain[ch]
                pool.wait_ge(sm["pay"], k + 1)
                if not isinstance(k, int) or k > 0:
                    pool.wait_ge(sm["scatter"], 16 * G * k)
                    pool.sem_inc(sm["landed"], 1)
                for g in range(tiles(k)):
                    nc.gpsimd.indirect_dma_start(
                        dest[:, :], bass.IndirectOffsetOnAxis(ap=target[c][off % 4][:, g:g + 1], axis=0),
                        pay[c][off % 4][:, g * F:(g + 1) * F], None, compute_op=ALU.add).then_inc(sm["scatter"], 16)

            def sums_step(i, off):
                for c in (0, 1):
                    scatter(c, agg[c], c, i, off)

            def shared_step(i, off):
                k, s, _ = at(i, off)
                reuse(pool, chain[1]["scatter"], 16 * G * k)
                scatter(0, agg_src, 0, i, off)
                pool.wait_ge(chain[0]["scatter"], 16 * G * k + 16 * G)
                scatter(1, agg_src, 1, i, off)

            pool.wait_ge(S["src_zeroed"], 32)
            for n in range(4):
                shared_step(0, n)
            with pool.Fori(1, SHARED // 4) as i:
                for n in range(4):
                    shared_step(i, n)
            pool.wait_ge(chain[1]["scatter"], 16 * G * SHARED)
            pool.wait_ge(S["dst_zeroed"], 16 * (2 * SHARED + 1))
            with pool.Fori(SHARED // 4, SB // 4) as i:
                for n in range(4):
                    sums_step(i, n)
            for k in range(SB // 4 * 4, SB + 1):
                sums_step(0, k)

            def prep(i, off):
                q, s, m = at(i, off)
                n = rows(q)
                pool.wait_ge(a_in[off % 4], 48 * (i + off // 4 + 1))
                reuse(pool, S["a_turned"], 3 * (q - 3))
                nc.gpsimd.tensor_tensor(xa[off % 4][0:n, :].rearrange("p (c f) -> p c f", c=C)[:, :, F:2 * F],
                                        v3(as_in[off % 4][0:n, :], n), v3(ad_in[off % 4][0:n, :], n), ALU.add)
                reuse(pool, S["a_res"], q - 3)
                nc.gpsimd.tensor_tensor(v3(xb[off % 4][0:n, :], n), v3(x_in[off % 4][0:n, :], n),
                                        b2r[0:n, :].unsqueeze(1).to_broadcast([n, C, F]),
                                        ALU.add).then_inc(S["a_prepped"], 1)

            def scale(pre, stored, per_store, i, off):
                q, s, m = at(i, off)
                n, c = size(pre, q)
                deviations, y = norm[pre]
                pool.wait_ge(S[pre + "rstd"], q + 1)
                reuse(pool, stored[off % 4], per_store * (i + off // 4))
                nc.gpsimd.tensor_tensor(v3(y[off % 4][0:n, 0:c * F], n), v3(deviations[off % 4][0:n, 0:c * F], n),
                                        rstd[off % 4][0:n, 0:c].unsqueeze(2).to_broadcast([n, c, F]),
                                        ALU.mult).then_inc(S[pre + "out"], 1)

            def dense_step(i, off):
                if exists(at(i, off)[0], CHUNKS):
                    prep(i, off)
                if exists(at(i, off - 4)[0], CHUNKS):
                    scale("a_", a_stored, 32, i, off - 4)

            pool.wait_ge(S["dense_consts"], 64)
            for n in range(8):
                dense_step(0, n)
            with pool.Fori(2, CHUNKS // 4) as i:
                for n in range(4):
                    dense_step(i, n)
            for q in range(CHUNKS // 4 * 4, CHUNKS + 5):
                dense_step(0, q)

            def gather(i, off):
                k, s, m = at(i, off)
                for g in range(tiles(k)):
                    n = TAIL if is_tail(k) and g == TF else P
                    nc.gpsimd.indirect_dma_start(
                        xg[off % 4][0:n, g * F:(g + 1) * F], None, x1[:, :],
                        bass.IndirectOffsetOnAxis(ap=gidx[off % 4][0:n, g:g + 1], axis=0)).then_inc(m_got[s], 16)

            def attend_step(i, off):
                k = at(i, off)[0]
                if exists(k, SB):
                    pool.wait_ge(S["m_gidx"], k + 1)
                if exists(at(i, off - 4)[0], SB):
                    scatter(2, acc, 0, i, off - 4)
                if exists(k, SB):
                    gather(i, off)

            for s in range(4):
                pool.wait_ge(a_stored[s], 32 * ((CHUNKS - s) // 4 + 1))
            for n in range(4):
                attend_step(0, n)
            with pool.Fori(1, SB // 4) as i:
                for n in range(4):
                    attend_step(i, n)
            for k in range(SB // 4 * 4, SB + 5):
                attend_step(0, k)

            def fold(i, off):
                q, s, _ = at(i, off)
                if not exists(q, LCHUNKS):
                    return
                n, c = size("f_", q)
                pool.wait_ge(f_in[off % 4], 16 * (i + off // 4 + 1))
                reuse(pool, S["f_sum"], q - 1)
                x3 = v3(last_in[off % 4][0:n, 0:c * F], n)
                nc.gpsimd.tensor_tensor(v3(folded[s][0:n, 0:c * F // 2], n, F // 2), x3[:, :, 0:F // 2], x3[:, :, F // 2:F],
                                        ALU.add).then_inc(S["f_fold"], 1)

            def last_step(i, off):
                fold(i, off + 1)
                if exists(at(i, off - 2)[0], LCHUNKS):
                    scale("f_", f_stored, 16, i, off - 2)

            fold(0, 0)
            for n in range(8):
                last_step(0, n)
            with pool.Fori(2, LCHUNKS // 4) as i:
                for n in range(4):
                    last_step(i, n)
            for q in range(LCHUNKS // 4 * 4, LCHUNKS + 3):
                last_step(0, q)

        @block.scalar
        def _(act):
            act.dma_start(w1[:, :], W1).then_inc(S["dense_consts"], 16)
            act.dma_start(w2[:, :], W2).then_inc(S["dense_consts"], 16)
            act.dma_start(b1c[:, :], b1.rearrange("(h o) -> h o", o=1)).then_inc(S["dense_consts"], 16)
            act.dma_start(b2r[:, :], b2.rearrange("(o f) -> o f", o=1).to_broadcast([P, F])).then_inc(S["dense_consts"], 16)
            act.wait_ge(S["wqkv_zero"], 1)
            for n, w in enumerate((Wq, Wk, Wv)):
                for h in range(HEADS):
                    act.dma_start(wqkv[h * FH:(h + 1) * FH, n * F + h * FH:n * F + (h + 1) * FH],
                                 w[h]).then_inc(S["wqkv_loaded"], 16)

            def stage_col(ch, c, i, off):
                k, s, _ = at(i, off)
                reuse(act, chain[ch]["target"], k - 3)
                nc.scalar.copy(col[c][off % 4][:, 0:tiles(k)], cols(idx_f[c], k)).then_inc(chain[ch]["col"], 1)

            def copy_pay(ch, c, i, off):
                k, s, _ = at(i, off)
                act.wait_ge(chain[ch]["sum"], k + 1)
                act.wait_ge(chain[ch]["target"], k + 1)
                reuse(act, chain[ch]["landed"], k - 3)
                w = tiles(k) * F
                nc.scalar.copy(pay[c][off % 4][:, 0:w], sum_ps[c][s][:, 0:w]).then_inc(chain[ch]["pay"], 1)

            def sums_step(i, off):
                for c in (0, 1):
                    if exists(at(i, off)[0], SB):
                        stage_col(c, c, i, off)
                for c in (0, 1):
                    if exists(at(i, off - 1)[0], SB):
                        copy_pay(c, c, i, off - 1)

            act.wait_ge(S["tables_made"], 1)
            for n in range(4):
                sums_step(0, n)
            with act.Fori(1, SB // 4) as i:
                for n in range(4):
                    sums_step(i, n)
            for k in range(SB // 4 * 4, SB + 2):
                sums_step(0, k)

            def copy_turned(i, n3):
                q, g, u = 4 * i + n3 // 3, n3 % 3, n3 % 2
                w = GROUPS[g][1] * rows(q)
                act.wait_ge(S["a_turned"], 3 * q + g + 1)
                reuse(act, S["a_h"], 3 * q + g - 1)
                nc.scalar.copy(xaT[u][:, 0:w], xaT_ps[u][:, 0:w]).then_inc(S["a_turn_sb"], 1)

            def relu(i, n3):
                q, g, u = 4 * i + n3 // 3, n3 % 3, n3 % 2
                if not exists(q, CHUNKS):
                    return
                w = GROUPS[g][1] * rows(q)
                act.wait_ge(S["a_h"], 3 * q + g + 1)
                reuse(act, S["a_y"], 3 * q + g - 1)
                nc.scalar.activation(hT[u][:, 0:w], h_ps[u][:, 0:w], ACT.Relu,
                                     bias=b1c[:, 0:1]).then_inc(S["a_h_sb"], 1)

            def square(pre, i, off):
                q, s, _ = at(i, off)
                if not exists(q, passes[pre][0]):
                    return
                n, c = size(pre, q)
                act.wait_ge(S[pre + "dev"], q + 1)
                reuse(act, S[pre + "sqsum"], q - 1)
                nc.scalar.activation(sq[s][0:n, 0:c * F], norm[pre][0][off % 4][0:n, 0:c * F],
                                     ACT.Square).then_inc(S[pre + "sq"], 1)

            def root(pre, i, off):
                q, s, _ = at(i, off)
                if not exists(q, passes[pre][0]):
                    return
                n, c = size(pre, q)
                act.wait_ge(S[pre + "sqsum"], q + 1)
                reuse(act, S[pre + "rstd"], q - 1)
                nc.scalar.activation(std[s][0:n, 0:c], sqsum[s][0:n, 0:c], ACT.Sqrt, scale=1.0 / F,
                                     bias=eps[0:n, 0:1]).then_inc(S[pre + "std"], 1)

            def store(pre, dests, stored, i, off):
                q, s, _ = at(i, off)
                if not exists(q, passes[pre][0]):
                    return
                act.wait_ge(S[pre + "out"], q + 1)
                n, c = size(pre, q)
                for dest in dests:
                    act.dma_start(chunk_of(pre, dest, q), norm[pre][1][off % 4][0:n, 0:c * F]).then_inc(stored[off % 4], 16)

            def dense_step(i, off):
                here = exists(at(i, off)[0], CHUNKS)
                for g in range(3):
                    if here:
                        copy_turned(i, 3 * off + g)
                    relu(i, 3 * off + g - 1)
                    if g == 0:
                        square("a_", i, off - 2)
                root("a_", i, off - 2)
                store("a_", (x1, acc), a_stored, i, off - 3)

            act.wait_ge(S["dense_consts"], 64)
            act.wait_ge(S["eps_made"], 1)
            for n in range(8):
                dense_step(0, n)
            with act.Fori(2, CHUNKS // 4) as i:
                for n in range(4):
                    dense_step(i, n)
            for q in range(CHUNKS // 4 * 4, CHUNKS + 4):
                dense_step(0, q)

            def stage_gather(i, off):
                k, s, m = at(i, off)
                reuse(act, m_got[s], 16 * G * m)
                reuse(act, S["m_turned"], k - 3)
                nc.scalar.copy(gidx[off % 4][:, 0:tiles(k)], cols(idx_f[1], k)).then_inc(S["m_gidx"], 1)

            def copy_turned_edges(i, off):
                k, s, _ = at(i, off)
                w = tiles(k)
                act.wait_ge(S["m_turned"], k + 1)
                reuse(act, S["m_qkv"], k - 1)
                nc.scalar.copy(xgT[s][:, 0:w * P], xgT_ps[s][:, 0:w * P]).then_inc(S["m_turn_sb"], 1)

            def copy_k(i, off):
                k, s, _ = at(i, off)
                w = tiles(k)
                act.wait_ge(S["m_qkv"], k + 1)
                reuse(act, S["m_qk"], k - 1)
                nc.scalar.copy(v3(k_sb[s][:, 0:w * F], P), qkv_ps[s][:, 0:w, F:2 * F]).then_inc(S["m_k_sb"], 1)

            def attend_step(i, off):
                if exists(at(i, off)[0], SB):
                    stage_col(2, 0, i, off)
                if exists(at(i, off + 2)[0], SB):
                    stage_gather(i, off + 2)
                if exists(at(i, off)[0], SB):
                    copy_turned_edges(i, off)
                if exists(at(i, off - 1)[0], SB):
                    copy_pay(2, 0, i, off - 1)
                if exists(at(i, off)[0], SB):
                    copy_k(i, off)

            stage_gather(0, 0)
            stage_gather(0, 1)
            for n in range(4):
                attend_step(0, n)
            with act.Fori(1, SB // 4 - 1) as i:
                for n in range(4):
                    attend_step(i, n)
            for k in range(SB // 4 * 4 - 4, SB + 2):
                attend_step(0, k)

            def last_step(i, off):
                square("f_", i, off)
                root("f_", i, off - 1)
                store("f_", (out,), f_stored, i, off - 3)

            for n in range(8):
                last_step(0, n)
            with act.Fori(2, LCHUNKS // 4) as i:
                for n in range(4):
                    last_step(i, n)
            for q in range(LCHUNKS // 4 * 4, LCHUNKS + 4):
                last_step(0, q)

        @block.tensor
        def _(pe):
            def turn_cols(ch, c, i, off):
                k, s, _ = at(i, off)
                pe.wait_ge(chain[ch]["col"], k + 1)
                reuse(pe, chain[ch]["same"], k - 1)
                for g in range(tiles(k)):
                    last = nc.tensor.transpose(row_ps[c][s][:, g * P:(g + 1) * P],
                                               col[c][off % 4][:, g:g + 1].to_broadcast([P, P]), ident[:, :])
                last.then_inc(chain[ch]["row"], 1)

            def sum_same(ch, c, i, off):
                k, s, _ = at(i, off)
                pe.wait_ge(chain[ch]["same"], k + 1)
                reuse(pe, chain[ch]["pay"], k - 1)
                for a in range(tiles(k)):
                    for b in range(a, tiles(k)):
                        at_b = b * G * P + a * P
                        for part in range(3):
                            last = nc.tensor.matmul(sum_ps[c][s][:, a * F:(a + 1) * F],
                                                    same[c][s][:, at_b:at_b + P],
                                                    parts[s][:, part, b * F:(b + 1) * F],
                                                    start=(b == a and part == 0),
                                                    stop=(b == tiles(k) - 1 and part == 2))
                last.then_inc(chain[ch]["sum"], 1)

            def sums_step(i, off):
                for c in (0, 1):
                    if exists(at(i, off)[0], SB):
                        turn_cols(c, c, i, off)
                if exists(at(i, off - 1)[0], SB):
                    pe.wait_ge(S["attr_split"], at(i, off - 1)[0] + 1)
                    for c in (0, 1):
                        sum_same(c, c, i, off - 1)

            pe.wait_ge(S["ident_made"], 1)
            for n in range(4):
                sums_step(0, n)
            with pe.Fori(1, SB // 4) as i:
                for n in range(4):
                    sums_step(i, n)
            for k in range(SB // 4 * 4, SB + 2):
                sums_step(0, k)

            def turn_nodes(i, n3):
                q, g, u = 4 * i + n3 // 3, n3 % 3, n3 % 2
                if not exists(q, CHUNKS):
                    return
                s, n = (n3 // 3) % 2, rows(q)
                if g == 0:
                    pe.wait_ge(S["a_x_copied"], q + 1)
                    pe.wait_ge(S["a_prepped"], q + 1)
                reuse(pe, S["a_turn_sb"], 3 * q + g - 1)
                c0, nc_ = GROUPS[g]
                for c in range(nc_):
                    last = nc.tensor.transpose(xaT_ps[u][:, c * n:(c + 1) * n],
                                               xa[n3 // 3 % 4][0:n, (c0 + c) * 2 * F:(c0 + c + 1) * 2 * F], ident[0:n, 0:n])
                last.then_inc(S["a_turned"], 1)

            def hidden(i, n3):
                q, g, u = 4 * i + n3 // 3, n3 % 3, n3 % 2
                if not exists(q, CHUNKS):
                    return
                w = GROUPS[g][1] * rows(q)
                pe.wait_ge(S["a_turn_sb"], 3 * q + g + 1)
                reuse(pe, S["a_h_sb"], 3 * q + g - 1)
                nc.tensor.matmul(h_ps[u][:, 0:w], w1[:, :], xaT[u][:, 0:w], start=True,
                                 stop=True).then_inc(S["a_h"], 1)

            def project(i, n3):
                q, g, u = 4 * i + n3 // 3, n3 % 3, n3 % 2
                if not exists(q, CHUNKS):
                    return
                s, n = (n3 // 3) % 2, rows(q)
                pe.wait_ge(S["a_h_sb"], 3 * q + g + 1)
                if g == 0:
                    reuse(pe, S["a_res"], q - 1)
                c0, nc_ = GROUPS[g]
                for c in range(nc_):
                    half, at_c = (c0 + c) // HALF, (c0 + c) % HALF * F
                    last = nc.tensor.matmul(y_ps[s][half][0:n, at_c:at_c + F], hT[u][:, c * n:(c + 1) * n],
                                            w2[:, :], start=True, stop=True)
                last.then_inc(S["a_y"], 1)

            def dense_step(i, off):
                for g in range(3):
                    turn_nodes(i, 3 * off + g)
                    hidden(i, 3 * off + g - 1)
                    project(i, 3 * off + g - 2)

            pe.wait_ge(S["dense_consts"], 64)
            for n in range(8):
                dense_step(0, n)
            with pe.Fori(2, CHUNKS // 4) as i:
                for n in range(4):
                    dense_step(i, n)
            for q in range(CHUNKS // 4 * 4, CHUNKS + 2):
                dense_step(0, q)

            def turn_edges(i, off):
                k, s, m = at(i, off)
                for g in range(tiles(k)):
                    last = nc.tensor.transpose(xgT_ps[s][:, g * P:(g + 1) * P], xg[off % 4][:, g * F:(g + 1) * F],
                                               ident[:, :])
                last.then_inc(S["m_turned"], 1)

            def project_edges(i, off):
                k, s, m = at(i, off)
                pe.wait_ge(S["m_turn_sb"], k + 1)
                for g in range(tiles(k)):
                    last = nc.tensor.matmul(qkv_ps[s][:, g, 0:3 * F], xgT[s][:, g * P:(g + 1) * P], wqkv[:, :],
                                            start=True, stop=True)
                last.then_inc(S["m_qkv"], 1)

            def attend_step(i, off):
                k, s, m = at(i, off)
                if exists(k, SB):
                    pe.wait_ge(m_got[s], 16 * G * m + 16 * tiles(k))
                    reuse(pe, S["m_msg"], k - 1)
                    turn_cols(2, 0, i, off)
                    turn_edges(i, off)
                if exists(at(i, off - 1)[0], SB):
                    pe.wait_ge(S["msg_split"], at(i, off - 1)[0] + 1)
                    sum_same(2, 0, i, off - 1)
                if exists(k, SB):
                    project_edges(i, off)

            pe.wait_ge(S["wqkv_loaded"], 16 * 3 * HEADS)
            for n in range(4):
                attend_step(0, n)
            with pe.Fori(1, SB // 4) as i:
                for n in range(4):
                    attend_step(i, n)
            for k in range(SB // 4 * 4, SB + 2):
                attend_step(0, k)

        @block.vector
        def _(dve):
            nc.vector.memset(zeros[:, :], 0.0).then_inc(S["zero_made"], 1)
            nc.vector.memset(wqkv[:, :], 0.0).then_inc(S["wqkv_zero"], 1)
            nc.vector.memset(eps[:, :], EPS).then_inc(S["eps_made"], 1)
            nc.vector.memset(weight[:, TL:TL + 1], 0.0)
            dve.wait_ge(S["spare_made"], 1)
            nc.vector.tensor_copy(spare_f[:, :], spare_i[:, :]).then_inc(S["table_step"], 1)
            dve.wait_ge(S["table_step"], 1)
            dve.wait_ge(S["idx_loaded"], 16 * 12)
            for c in (0, 1):
                nc.vector.tensor_copy(idx_f[c][:, 0:TL], idx_i[c][:, 0:TL])
                nc.vector.tensor_copy(idx_f[c][:, TL:TL + 1], spare_f[:, TF:TF + 1]).then_inc(S["table_step"], 1)
            dve.wait_ge(S["table_step"], 3)
            for c in (0, 1):
                nc.vector.tensor_copy(idx_f[c][0:TAIL, TL:TL + 1],
                                      idx_i[c][0:TAIL, TL:TL + 1]).then_inc(S["table_step"], 1)
            for n, lo, hi in ((P, 0, TL), (TAIL, TL, TL + 1)):
                nc.vector.scalar_tensor_tensor(out=weight[0:n, lo:hi], in0=ew[0:n, lo:hi], scalar=float(FH) ** -0.5,
                                               in1=ew2[0:n, lo:hi], op0=ALU.mult, op1=ALU.mult)
            dve.wait_ge(S["table_step"], 5)
            for c in (0, 1):
                nc.vector.tensor_tensor(to_spare[c][:, 0:T].rearrange("p (k g) -> p k g", g=G),
                                        spare_f[:, :].unsqueeze(1).to_broadcast([P, SB, G]),
                                        idx_f[c][:, 0:T].rearrange("p (k g) -> p k g", g=G), ALU.subtract)
                last = nc.vector.tensor_tensor(to_spare[c][:, T:TL + 1], spare_f[:, 0:TF + 1],
                                               idx_f[c][:, T:TL + 1], ALU.subtract)
            last.then_inc(S["tables_made"], 1)
            dve.wait_ge(S["tables_made"], 1)
            dve.wait_ge(S["mask_made"], 1)

            def compare(ch, c, i, off):
                k, s, _ = at(i, off)
                sm, t = chain[ch], tiles(k)
                dve.wait_ge(sm["row"], k + 1)
                reuse(dve, sm["sum"], k - 1)
                for b in range(t):
                    w = (b + 1) * P
                    last = nc.vector.scalar_tensor_tensor(
                        out=same[c][s][:, b * G * P:b * G * P + w], in0=row_ps[c][s][:, 0:w],
                        scalar=col[c][off % 4][:, b:b + 1], in1=earlier[:, G * P - w:G * P],
                        op0=ALU.is_equal, op1=ALU.mult, accum_out=rank[c][s][:, b:b + 1])
                last.then_inc(sm["same"], 1)
                dve.wait_ge(sm["same"], k + 1)
                nc.vector.scalar_tensor_tensor(out=move[c][off % 4][:, 0:t], in0=rank[c][s][:, 0:t], scalar=1.5,
                                               in1=cols(to_spare[c], k), op0=ALU.is_gt,
                                               op1=ALU.mult).then_inc(sm["moved"], 1)
                dve.wait_ge(sm["moved"], k + 1)
                reuse(dve, sm["landed"], k - 3)
                nc.vector.tensor_tensor(target[c][off % 4][:, 0:t], move[c][off % 4][:, 0:t], col[c][off % 4][:, 0:t],
                                        ALU.add).then_inc(sm["target"], 1)

            def split(name, value, i, off):
                k, s, _ = at(i, off)
                w = tiles(k) * F
                high, mid, low = (parts[s][:, part, 0:w] for part in range(3))
                nc.vector.tensor_copy(high, value[s][:, 0:w]).then_inc(S[name + "_high"], 1)
                dve.wait_ge(S[name + "_high"], k + 1)
                nc.vector.tensor_tensor(left[s][:, 0:w], value[s][:, 0:w], high, ALU.subtract).then_inc(S[name + "_left"], 1)
                dve.wait_ge(S[name + "_left"], k + 1)
                nc.vector.tensor_copy(mid, left[s][:, 0:w]).then_inc(S[name + "_mid"], 1)
                dve.wait_ge(S[name + "_mid"], k + 1)
                nc.vector.tensor_tensor(low, left[s][:, 0:w], mid, ALU.subtract).then_inc(S[name + "_split"], 1)

            def sums_step(i, off):
                k, s, m = at(i, off)
                dve.wait_ge(attr_in[s], 16 * (m + 1) + 16 * is_tail(k))
                for c in (0, 1):
                    reuse(dve, chain[c]["sum"], k - 1)
                split("attr", attr, i, off)
                for c in (0, 1):
                    compare(c, c, i, off)

            for n in range(4):
                sums_step(0, n)
            with dve.Fori(1, SB // 4) as i:
                for n in range(4):
                    sums_step(i, n)
            for k in range(SB // 4 * 4, SB + 1):
                sums_step(0, k)

            def deviate(pre, value, summed, width, i, off):
                q, s, _ = at(i, off)
                n, c = size(pre, q)
                nc.vector.tensor_reduce(total[s][0:n, 0:c], v3(summed[0:n, 0:c * width], n, width), AX_X,
                                        ALU.add).then_inc(S[pre + "sum"], 1)
                dve.wait_ge(S[pre + "sum"], q + 1)
                reuse(dve, S[pre + "out"], q - 3)
                nc.vector.scalar_tensor_tensor(out=v3(norm[pre][0][off % 4][0:n, 0:c * F], n),
                                               in0=total[s][0:n, 0:c].unsqueeze(2).to_broadcast([n, c, F]),
                                               scalar=-1.0 / F, in1=v3(value[0:n, 0:c * F], n), op0=ALU.mult,
                                               op1=ALU.add).then_inc(S[pre + "dev"], 1)

            def sum_squares(pre, i, off):
                q, s, _ = at(i, off)
                if not exists(q, passes[pre][0]):
                    return
                n, c = size(pre, q)
                dve.wait_ge(S[pre + "sq"], q + 1)
                nc.vector.tensor_reduce(sqsum[s][0:n, 0:c], v3(sq[s][0:n, 0:c * F], n), AX_X,
                                        ALU.add).then_inc(S[pre + "sqsum"], 1)

            def invert(pre, i, off):
                q, s, _ = at(i, off)
                if not exists(q, passes[pre][0]):
                    return
                n, c = size(pre, q)
                dve.wait_ge(S[pre + "std"], q + 1)
                reuse(dve, S[pre + "out"], q - 3)
                nc.vector.reciprocal(rstd[off % 4][0:n, 0:c], std[s][0:n, 0:c]).then_inc(S[pre + "rstd"], 1)

            def copy_x(i, off):
                q, s, m = at(i, off)
                n = rows(q)
                dve.wait_ge(a_in[off % 4], 48 * (i + off // 4 + 1))
                reuse(dve, S["a_turned"], 3 * (q - 3))
                nc.vector.tensor_copy(xa[off % 4][0:n, :].rearrange("p (c f) -> p c f", c=C)[:, :, 0:F],
                               v3(x_in[off % 4][0:n, :], n)).then_inc(S["a_x_copied"], 1)

            def dense_step(i, off):
                if exists(at(i, off + 2)[0], CHUNKS):
                    copy_x(i, off + 2)
                sum_squares("a_", i, off - 1)
                q, s, _ = at(i, off)
                if exists(q, CHUNKS):
                    n = rows(q)
                    dve.wait_ge(S["a_prepped"], q + 1)
                    dve.wait_ge(S["a_y"], 3 * q + 3)
                    for half in (0, 1):
                        lo = half * HALF * F
                        last = nc.vector.tensor_tensor(res[s][0:n, lo:lo + HALF * F], y_ps[s][half][0:n, 0:HALF * F],
                                                       xb[off % 4][0:n, lo:lo + HALF * F], ALU.add)
                    last.then_inc(S["a_res"], 1)
                    dve.wait_ge(S["a_res"], q + 1)
                    deviate("a_", res[s], res[s], F, i, off)
                invert("a_", i, off - 1)

            copy_x(0, 0)
            copy_x(0, 1)

            for n in range(8):
                dense_step(0, n)
            with dve.Fori(2, CHUNKS // 4) as i:
                for n in range(4):
                    dense_step(i, n)
            for q in range(CHUNKS // 4 * 4, CHUNKS + 2):
                dense_step(0, q)

            def message(i, off):
                k, s, _ = at(i, off)
                t = tiles(k)
                dve.wait_ge(S["m_k_sb"], k + 1)
                nc.vector.tensor_tensor(v3(qk[s][:, 0:t * F], P),
                                        qkv_ps[s][:, 0:t, 0:F],
                                        v3(k_sb[s][:, 0:t * F], P), ALU.mult).then_inc(S["m_qk"], 1)
                dve.wait_ge(S["m_qk"], k + 1)
                nc.vector.tensor_reduce(alpha[s][:, 0:t * HEADS],
                                        qk[s][:, 0:t * F].rearrange("p (h f) -> p h f", f=FH), AX_X,
                                        ALU.add).then_inc(S["m_alpha"], 1)
                dve.wait_ge(S["m_alpha"], k + 1)
                nc.vector.tensor_tensor(alpha_w[s][:, 0:t * HEADS].rearrange("p (g h) -> p g h", h=HEADS),
                                        alpha[s][:, 0:t * HEADS].rearrange("p (g h) -> p g h", h=HEADS),
                                        cols(weight, k).unsqueeze(2).to_broadcast([P, t, HEADS]),
                                        ALU.mult).then_inc(S["m_alpha_w"], 1)
                dve.wait_ge(S["m_alpha_w"], k + 1)
                nc.vector.tensor_tensor(msg[s][:, 0:t * F].rearrange("p (g h f) -> p g h f", g=t, f=FH),
                                        qkv_ps[s][:, 0:t, 2 * F:3 * F].rearrange("p g (h f) -> p g h f", f=FH),
                                        alpha_w[s][:, 0:t * HEADS].rearrange("p (g h) -> p g h", h=HEADS)
                                        .unsqueeze(3).to_broadcast([P, t, HEADS, FH]),
                                        ALU.mult).then_inc(S["m_msg"], 1)

            def attend_step(i, off):
                compare(2, 0, i, off)
                message(i, off)
                dve.wait_ge(S["m_msg"], at(i, off)[0] + 1)
                split("msg", msg, i, off)

            for n in range(4):
                attend_step(0, n)
            with dve.Fori(1, SB // 4) as i:
                for n in range(4):
                    attend_step(i, n)
            for k in range(SB // 4 * 4, SB + 1):
                attend_step(0, k)

            def last_step(i, off):
                q, s, m = at(i, off)
                if exists(q, LCHUNKS):
                    dve.wait_ge(f_in[off % 4], 16 * (i + off // 4 + 1))
                    dve.wait_ge(S["f_fold"], q + 1)
                    deviate("f_", last_in[off % 4], folded[s], F // 2, i, off)
                sum_squares("f_", i, off - 1)
                invert("f_", i, off - 2)

            for n in range(8):
                last_step(0, n)
            with dve.Fori(2, LCHUNKS // 4) as i:
                for n in range(4):
                    last_step(i, n)
            for q in range(LCHUNKS // 4 * 4, LCHUNKS + 3):
                last_step(0, q)


_INS = ["x", "src", "dst", "edge_attr_64", "edge_weight", "edge_weight_n2", "L0_gnn_W1", "L0_gnn_b1", "L0_gnn_W2",
        "L0_gnn_b2", "L1_gnn_Wq", "L1_gnn_Wk", "L1_gnn_Wv"]


def kernel(**inputs):
    import numpy as _np
    import concourse.bacc as _bacc
    from concourse import mybir as _mybir
    from concourse.bass_utils import run_bass_kernel_spmd as _run

    nc = _bacc.Bacc("TRN2", target_bir_lowering=False, num_devices=1)
    arrays, args = {}, []
    for name in _INS:
        a = _np.ascontiguousarray(inputs[name])
        arrays[f"in_{name}"] = a
        args.append(nc.dram_tensor(f"in_{name}", a.shape, _mybir.dt.from_np(a.dtype), kind="ExternalInput").ap())
    out = nc.dram_tensor("out_0", inputs["x"].shape, _mybir.dt.float32, kind="ExternalOutput").ap()
    build(nc, *args, out)
    r = _run(nc, [arrays], core_ids=[0])
    return r.results[0]["out_0"]
```
